# Optimizing a Trainium2 kernel written in Bass

```python
import numpy as np
import jax
import jax.numpy as jnp

def _softmax(x, axis=-1):
    return jax.nn.softmax(x, axis=axis)

def _gelu(x):
    return jax.nn.gelu(x, approximate=True)

def _silu(x):
    return jax.nn.silu(x)

def _sigmoid(x):
    return jax.nn.sigmoid(x)

def _layernorm(x, axis=-1, eps=1e-05):
    m = jnp.mean(x, axis=axis, keepdims=True)
    v = jnp.var(x, axis=axis, keepdims=True)
    return (x - m) / jnp.sqrt(v + eps)

def _scatter_add(tgt, idx, src, axis=0):
    return tgt.at[idx].add(src)

def _segment_sum(src, seg, n):
    return jax.ops.segment_sum(src, seg, n)
kernel_name = 'mk_adaln_ffn_d2_seqx_r8_c98f4c'

def setup_inputs(seed: int=0):
    np.random.seed(seed)
    _w = jnp.asarray

    def _rec_inputs():
        import jax
        import jax.numpy as jnp
        _rk = jax.random.key(seed)
        x = -7.109e-05 + 0.9999 * jax.random.normal(jax.random.fold_in(_rk, 1), (16, 128, 128), jnp.float32)
        _lenS = 128 - jax.random.randint(jax.random.fold_in(_rk, 7), (16,), 0, max(1, 128 // 4) + 1, jnp.int32)
        _lenS2 = 128 - jax.random.randint(jax.random.fold_in(_rk, 8), (16,), 0, max(1, 128 // 4) + 1, jnp.int32)
        cond_1024 = 0.00386106 + 1.00199 * jax.random.normal(jax.random.fold_in(_rk, 11), (16, 128), jnp.float32)
        return (x, cond_1024)
    x, cond_1024 = _rec_inputs()

    def _L0_cond_setup():
        import jax, jax.numpy as jnp
        import numpy as np
        import math
        IN_F = 128
        OUT_F = 128
        B = 16
        L = 512
        key = jax.random.key(seed)
        k1, k2, k3 = jax.random.split(key, 3)
        Efou = jax.random.normal(k1, (B, L, IN_F), dtype=jnp.float32)
        y = jax.random.normal(k2, (B, IN_F), dtype=jnp.float32)
        weight = jax.random.normal(k3, (1, OUT_F, IN_F, 1), dtype=jnp.float32)
        return {'Efou': Efou, 'y': y, 'weight': weight}
    _L0_cond_all = _L0_cond_setup()
    _L0_cond_in = {k: v for k, v in _L0_cond_all.items() if k in ('weight',)}
    del _L0_cond_all

    def _L0_ffn_setup():
        import jax, jax.numpy as jnp
        import numpy as np
        BLOCK = 32
        W_BITS = 4
        ACT_BITS = 16

        def act_qdq(x):
            qmax = 2.0 ** (ACT_BITS - 1) - 1.0
            scale = jnp.maximum(jnp.max(jnp.abs(x)) / qmax, 1e-12)
            return jnp.clip(jnp.round(x / scale), -qmax - 1.0, qmax) * scale

        def fixed_qdq_u16(x):
            scale = 1.0 / 65536.0
            return jnp.clip(jnp.round(x / scale), 0.0, 65535.0) * scale

        def lpbq_dequant(w):
            O, I = w.shape
            qmax = 2.0 ** (W_BITS - 1) - 1.0
            wb = w.reshape(O, I // BLOCK, BLOCK)
            s = jnp.maximum(jnp.max(jnp.abs(wb), axis=-1, keepdims=True) / qmax, 1e-12)
            wq = jnp.clip(jnp.round(wb / s), -qmax - 1.0, qmax) * s
            return wq.reshape(O, I)
        key = jax.random.key(seed)
        k1, k2, k3, k4 = jax.random.split(key, 4)
        B, S, H, I = (2, 512, 128, 384)
        x = jax.random.normal(k1, (B, S, H), jnp.float32)
        w_gate = jax.random.normal(k2, (I, H), jnp.float32) * 0.02
        w_up = jax.random.normal(k3, (I, H), jnp.float32) * 0.02
        w_down = jax.random.normal(k4, (H, I), jnp.float32) * 0.02
        return {'x': x, 'w_gate': w_gate, 'w_up': w_up, 'w_down': w_down}
    _L0_ffn_all = _L0_ffn_setup()
    _L0_ffn_in = {k: v for k, v in _L0_ffn_all.items() if k in ('w_gate', 'w_up', 'w_down')}
    del _L0_ffn_all

    def _L1_cond_setup():
        import jax, jax.numpy as jnp
        import numpy as np
        N, T, D, H = (64, 64, 128, 128)
        key = jax.random.key(seed)
        k1, k2, k3, k4 = jax.random.split(key, 4)
        x = jax.random.normal(k1, (N, T, D), dtype=jnp.float32)
        h0 = jax.random.normal(k2, (N, H), dtype=jnp.float32)
        Wx = jax.random.normal(k3, (D, H), dtype=jnp.float32) / jnp.sqrt(jnp.float32(D))
        Wh = jax.random.normal(k4, (H, H), dtype=jnp.float32) / jnp.sqrt(jnp.float32(H))
        b = jnp.zeros((H,), dtype=jnp.float32)
        return {'x': x, 'h0': h0, 'Wx': Wx, 'Wh': Wh, 'b': b}
    _L1_cond_all = _L1_cond_setup()
    _L1_cond_in = {k: v for k, v in _L1_cond_all.items() if k in ('Wx', 'Wh', 'b')}
    del _L1_cond_all

    def _L1_ffn_setup():
        import jax, jax.numpy as jnp
        import numpy as np
        TOP_K = 2
        key = jax.random.key(seed)
        ks = jax.random.split(key, 6)
        B, T, H, E, F = (2, 256, 128, 8, 512)
        s = 0.02
        return {'hidden_states': jax.random.normal(ks[0], (B, T, H), dtype=jnp.float32), 'router_w': jax.random.normal(ks[1], (E, H), dtype=jnp.float32) * s, 'w1': jax.random.normal(ks[2], (E, F, H), dtype=jnp.float32) * s, 'b1': jax.random.normal(ks[3], (E, F), dtype=jnp.float32) * s, 'w2': jax.random.normal(ks[4], (E, H, F), dtype=jnp.float32) * s, 'b2': jax.random.normal(ks[5], (E, H), dtype=jnp.float32) * s}
    _L1_ffn_all = _L1_ffn_setup()
    _L1_ffn_in = {k: v for k, v in _L1_ffn_all.items() if k in ('router_w', 'w1', 'b1', 'w2', 'b2')}
    del _L1_ffn_all
    return {'x': x, 'cond_1024': cond_1024, 'L0_cond_weight': _L0_cond_in['weight'], 'L0_ffn_w_gate': _L0_ffn_in['w_gate'], 'L0_ffn_w_up': _L0_ffn_in['w_up'], 'L0_ffn_w_down': _L0_ffn_in['w_down'], 'L1_cond_Wx': _L1_cond_in['Wx'], 'L1_cond_Wh': _L1_cond_in['Wh'], 'L1_cond_b': _L1_cond_in['b'], 'L1_ffn_router_w': _L1_ffn_in['router_w'], 'L1_ffn_w1': _L1_ffn_in['w1'], 'L1_ffn_b1': _L1_ffn_in['b1'], 'L1_ffn_w2': _L1_ffn_in['w2'], 'L1_ffn_b2': _L1_ffn_in['b2']}

def reference(x, cond_1024, L0_cond_weight, L0_ffn_w_gate, L0_ffn_w_up, L0_ffn_w_down, L1_cond_Wx, L1_cond_Wh, L1_cond_b, L1_ffn_router_w, L1_ffn_w1, L1_ffn_b1, L1_ffn_w2, L1_ffn_b2):
    import jax
    import jax.numpy as jnp

    def _L0_cond_ref(Efou, y, weight):
        import jax, jax.numpy as jnp
        import numpy as np
        import math
        IN_F = 128
        OUT_F = 128
        B = 16
        L = 512
        b, img_size, in_f = Efou.shape
        out_f = weight.shape[1]
        scale = 1.0 / math.sqrt(in_f)
        w = scale * weight[:, :, :, 0] * y[:, None, :]
        dnorm = jax.lax.rsqrt(jnp.sum(w * w, axis=2, keepdims=True) + 1e-08)
        w = w * dnorm
        E = Efou.reshape(b, in_f, img_size)
        x = jnp.einsum('boi,bil->bol', w, E)
        return x.reshape(b, img_size, out_f)

    def _L0_ffn_ref(x, w_gate, w_up, w_down):
        import jax, jax.numpy as jnp
        import numpy as np
        BLOCK = 32
        W_BITS = 4
        ACT_BITS = 16

        def act_qdq(x):
            qmax = 2.0 ** (ACT_BITS - 1) - 1.0
            scale = jnp.maximum(jnp.max(jnp.abs(x)) / qmax, 1e-12)
            return jnp.clip(jnp.round(x / scale), -qmax - 1.0, qmax) * scale

        def fixed_qdq_u16(x):
            scale = 1.0 / 65536.0
            return jnp.clip(jnp.round(x / scale), 0.0, 65535.0) * scale

        def lpbq_dequant(w):
            O, I = w.shape
            qmax = 2.0 ** (W_BITS - 1) - 1.0
            wb = w.reshape(O, I // BLOCK, BLOCK)
            s = jnp.maximum(jnp.max(jnp.abs(wb), axis=-1, keepdims=True) / qmax, 1e-12)
            wq = jnp.clip(jnp.round(wb / s), -qmax - 1.0, qmax) * s
            return wq.reshape(O, I)
        x = act_qdq(x)
        up = act_qdq(x @ lpbq_dequant(w_up).T)
        gate = act_qdq(x @ lpbq_dequant(w_gate).T)
        sig = fixed_qdq_u16(jax.nn.sigmoid(gate))
        gate = act_qdq(gate * sig)
        o = act_qdq(gate * up)
        return o @ lpbq_dequant(w_down).T

    def _L1_cond_ref(x, h0, Wx, Wh, b):
        import jax, jax.numpy as jnp
        import numpy as np
        N, T, D, H = (64, 64, 128, 128)
        xw = jnp.einsum('ntd,dh->nth', x, Wx) + b

        def step(prev_h, xw_t):
            next_h = jnp.tanh(xw_t + prev_h @ Wh)
            return (next_h, next_h)
        _, hs = jax.lax.scan(step, h0, jnp.swapaxes(xw, 0, 1))
        return jnp.swapaxes(hs, 0, 1)

    def _L1_ffn_ref(hidden_states, router_w, w1, b1, w2, b2):
        import jax, jax.numpy as jnp
        import numpy as np
        TOP_K = 2
        x = hidden_states
        router_logits = jnp.einsum('bth,eh->bte', x, router_w)
        topk_values, topk_indices = jax.lax.top_k(router_logits, TOP_K)
        topk_weights = jax.nn.softmax(topk_values.astype(jnp.float32), axis=-1).astype(x.dtype)
        h1 = jnp.einsum('bth,efh->btef', x, w1) + b1
        h1 = jax.nn.gelu(h1, approximate=False)
        expert_outputs = jnp.einsum('btef,ehf->bteh', h1, w2) + b2
        gather_idx = topk_indices[..., None]
        topk_expert_outputs = jnp.take_along_axis(expert_outputs, gather_idx, axis=2)
        mixed_output = jnp.sum(topk_expert_outputs * topk_weights[..., None], axis=2)
        return mixed_output
    x = x + _L0_ffn_ref(_L0_cond_ref(x, cond_1024, L0_cond_weight), L0_ffn_w_gate, L0_ffn_w_up, L0_ffn_w_down)
    x = x + _L1_ffn_ref(_L1_cond_ref(x, cond_1024, L1_cond_Wx, L1_cond_Wh, L1_cond_b), L1_ffn_router_w, L1_ffn_w1, L1_ffn_b1, L1_ffn_w2, L1_ffn_b2)
    return x

_drawn_inputs = setup_inputs


def setup_inputs(seed=0):
    import zlib

    import numpy as np

    out = dict(_drawn_inputs(seed))
    spreads = {'L1_cond_b': (0.0, 2.0)}
    factors = {'cond_1024': 4.898,
     'L0_cond_weight': 5.154,
     'L0_ffn_w_gate': 5.184,
     'L0_ffn_w_up': 5.039,
     'L0_ffn_w_down': 5.1,
     'L1_ffn_b1': 33.497,
     'L1_ffn_b2': 3.896,
     'L1_ffn_w1': 3.678,
     'L1_ffn_w2': 2.778}
    for name, (base, spread) in spreads.items():
        noise = np.random.default_rng([zlib.crc32(name.encode()), seed]).standard_normal(out[name].shape)
        drawn = base * np.exp(spread * noise) if base else spread * noise
        out[name] = jnp.asarray(drawn.astype(out[name].dtype))
    for name, factor in factors.items():
        out[name] = (out[name] * factor).astype(out[name].dtype)
    return out
```

```python
from contextlib import ExitStack

import concourse.bass as bass
from concourse import mybir

F32, F16 = mybir.dt.float32, mybir.dt.float16
I16, U16 = mybir.dt.int16, mybir.dt.uint16
ALU = mybir.AluOpType
ACT = mybir.ActivationFunctionType
X = mybir.AxisListType.X

P = 128
B = 16
T = 128
TOK = B * T
INNER = 384
NJ = INNER // P
BANK = 512
NK = TOK // BANK
WBLK = 32
NW = 3 * NJ
E, FF = 8, 512
NF = FF // P
STEPS = BANK // B
CH = T // STEPS
TILES = BANK // P
SLOTS = E * NF
WS = 256.0
QMAX = 32767.0
TINY = 1e-12
MAGIC = 12582912.0
SIG_MAGIC = 192.0
SIG_MAX = 65535.0 / 65536.0


def program(nc, x, cond, w_cond, w_gate, w_up, w_down, w_x, w_h, b_h, w_router, w1, b1, w2, b2, out):
    ctx = ExitStack()
    with ctx:
        def sb(name, shape, dt=F32):
            return ctx.enter_context(nc.sbuf_tensor(name, shape, dt))

        def sem(name):
            return ctx.enter_context(nc.semaphore(name))

        banks = [ctx.enter_context(nc.psum_tensor(f"bank{i}", [P, BANK], F32)) for i in range(8)]

        ident = sb("ident", [P, P])
        ident16 = sb("ident16", [P, P], F16)
        ones = sb("ones", [1, P])
        ones16 = sb("ones16", [1, P], F16)
        experts = sb("experts", [P, E])
        x_sb = sb("x_sb", [P, B, P])
        xT = sb("xT", [P, B, T])
        wc = sb("wc", [P, P])
        y_sb = sb("y_sb", [B, P])
        wcT = sb("wcT", [P, P])
        yT = sb("yT", [P, B])
        wc2 = sb("wc2", [P, P])
        y2 = sb("y2", [P, B])
        nrm = sb("nrm", [P, 5, B])
        wyT = sb("wyT", [P, B, P])
        c32 = sb("c32", [P, B, P])
        qhi = sb("qhi", [P, TOK], F16)
        qlo = sb("qlo", [P, TOK], F16)
        wn = sb("wn", [P, NW, P])
        ws = sb("ws", [P, 2, NW * P // WBLK])
        wT_hi = sb("wT_hi", [P, NW, P], F16)
        wT_lo = sb("wT_lo", [P, NW, P], F16)
        big = sb("big", [P, 3 * NJ * TOK])
        gate, up, sig = (big[:, i * NJ * TOK:(i + 1) * NJ * TOK].rearrange("p (j n) -> p j n", j=NJ) for i in range(3))
        peak = sb("peak", [P, 5, NJ * NK])
        pk1 = sb("pk1", [P, 5])
        pk0 = sb("pk0", [1, 5])
        sc = sb("sc", [P, 5, 5])
        x1 = c32[:, :, :].rearrange("p b l -> p (b l)").rearrange("p (t b) -> p t b", b=B)
        x1_hi, x1_lo = (x_sb[:, :, :].rearrange("p b l -> p (b l)").bitcast(F16)[:, i * TOK:(i + 1) * TOK] for i in range(2))
        acc = wyT
        wxh = sb("wxh", [P, 2, P])
        wxh_hi = sb("wxh_hi", [P, 2, P], F16)
        wxh_lo = sb("wxh_lo", [P, 2, P], F16)
        NM = E * NF + 1 + E
        misc = sb("misc", [NM, P])
        miscT = sb("miscT", [P, NM])
        rw_hi = sb("rw_hi", [P, E], F16)
        rw_lo = sb("rw_lo", [P, E], F16)
        b2row = sb("b2row", [1, E * P])
        b2_hi = sb("b2_hi", [1, E, P], F16)
        b2_lo = sb("b2_lo", [1, E, P], F16)
        stage = sb("stage", [P, 2, 4 * BANK])
        nat = sb("nat", [P, 4, SLOTS * P], F16)
        h_hi = sb("h_hi", [P, TOK + B], F16)
        h_lo = sb("h_lo", [P, TOK + B], F16)
        h32 = sb("h32", [P, 4, B])
        wt = big[:, :].bitcast(F16)[:, 0:4 * SLOTS * P].rearrange("p (a n) -> p a n", a=4)
        sigf = big[:, 2 * NJ * TOK:3 * NJ * TOK]
        g32 = sigf[:, 0:4 * BANK].rearrange("p (f n) -> p f n", f=NF)
        g_hi, g_lo = (sigf.bitcast(F16)[:, 8 * BANK * (i + 1):8 * BANK * (i + 2)].rearrange("p (a f n) -> p a f n", a=2, f=NF)
                      for i in range(2))
        top = sb("top", [P, TILES, 8])
        logit = sb("logit", [P, TILES, E])
        topi = sb("topi", [P, TILES, 8], U16)
        mixd = sb("mixd", [P, 4, TILES])
        pick = sb("pick", [P, 2, TILES, E])
        gates = sb("gates", [P, CH * TILES, E])

        ld_cond, ld_x, ld_w0, ld_misc, ld_wx, ld_b2 = (sem(n) for n in
            ("ld_cond", "ld_x", "ld_w0", "ld_misc", "ld_wx", "ld_b2"))
        ld_stage = [sem("ld_stage0"), sem("ld_stage1")]
        consts, cond_T, cond_sb, norm_in, norm_mm, norm_sb, root_done = (sem(n) for n in
            ("consts", "cond_T", "cond_sb", "norm_in", "norm_mm", "norm_sb", "root_done"))
        xT_mm, xT_sb, wy_done, c_mm, c_sb, cq_done, cT_mm, q_hi_done, q_done = (sem(n) for n in
            ("xT_mm", "xT_sb", "wy_done", "c_mm", "c_sb", "cq_done", "cT_mm", "q_hi_done", "q_done"))
        wdeq, wT_mm, wT_hi_done, wT_done = (sem(n) for n in ("wdeq", "wT_mm", "wT_hi_done", "wT_done"))
        misc_T, misc_sb = sem("misc_T"), sem("misc_sb")
        pk_part, pk_row, pk_one, pk_all, scale_done = (sem(n) for n in
            ("pk_part", "pk_row", "pk_one", "pk_all", "scale_done"))
        gu_mm, gu_sb, gateq, upq, sig_done, g2_done, g2q, p_done, oq, o_hi_done, o_done = (sem(n) for n in
            ("gu_mm", "gu_sb", "gateq", "upq", "sig_done", "g2_done", "g2q", "p_done", "oq", "o_hi_done", "o_done"))
        down_mm, x1_done, x1_hi_done, x1_lo_done, x1T_mm, added = (sem(n) for n in
            ("down_mm", "x1_done", "x1_hi_done", "x1_lo_done", "x1T_mm", "added"))
        nat_done, pool_step, small_w, nat_T, wt_done = (sem(n) for n in
            ("nat_done", "pool_step", "small_w", "nat_T", "wt_done"))
        dve_step = sem("dve_step")
        rnn_mm, h_hi_done, h32_done, h_lo_done = (sem(n) for n in ("rnn_mm", "h_hi_done", "h32_done", "h_lo_done"))
        logits_mm, logit_sb, top_done, margin_done, mix_done, pick_done, gates_done = (sem(n) for n in
            ("logits_mm", "logit_sb", "top_done", "margin_done", "mix_done", "pick_done", "gates_done"))
        up_mm, g_hi_done, g32_done, g_lo_done, y_mm, stored = (sem(n) for n in
            ("up_mm", "g_hi_done", "g32_done", "g_lo_done", "y_mm", "stored"))

        ps_rnn = [banks[0], banks[3]]
        ps_y = [banks[1], banks[2]]
        ps_pk = banks[7]
        ps_h = banks[4:8]
        ps_logits = ps_h[NF - 1]
        w1T_hi, w1T_lo, w2T_hi, w2T_lo = (wt[:, i, :] for i in range(4))

        def q16(t, dt=I16):
            return t.bitcast(dt)[:, 0::2]

        gate2, up2, sig2 = (t[:, :, :].rearrange("p j n -> p (j n)") for t in (gate, up, sig))
        o_hi = gate2.bitcast(F16)[:, 0:NJ * TOK]
        o_lo = gate2.bitcast(F16)[:, NJ * TOK:2 * NJ * TOK]
        GB = 6
        WB = 3

        def blk(t, n):
            return t[:, BANK * n:BANK * (n + 1)]

        def chunks(eng, pair):
            def chunk(c, prev, rnn):
                pair(c, 0, prev, rnn)
                with eng.Fori(1, E // 2) as e2:
                    pair(c, e2, True, rnn)
            chunk(0, False, True)
            with eng.Fori(1, CH - 1) as c:
                chunk(c, True, True)
            chunk(CH - 1, True, False)

        block = ctx.enter_context(nc.Block())

        @block.sync
        def _(sp):
            sp.dma_start(wc[:, :], w_cond.rearrange("a o i c -> (a o) (i c)")).then_inc(ld_cond, 16)
            sp.dma_start(y_sb[:, :], cond).then_inc(ld_cond, 16)
            for h in range(2):
                sp.dma_start(x_sb[:, 8 * h:8 * h + 8, :],
                             x[8 * h:8 * h + 8].rearrange("b p l -> p b l")).then_inc(ld_x, 16)
            sp.dma_start(wn[:, 0:NJ, :], w_gate.rearrange("(j p) i -> p j i", p=P)).then_inc(ld_w0, 16)
            sp.dma_start(wn[:, NJ:2 * NJ, :], w_up.rearrange("(j p) i -> p j i", p=P)).then_inc(ld_w0, 16)
            sp.dma_start(wn[:, 2 * NJ:NW, :], w_down.rearrange("p (j i) -> p j i", j=NJ)).then_inc(ld_w0, 16)
            sp.dma_start(wxh[:, 0, :], w_x).then_inc(ld_wx, 16)
            sp.dma_start(wxh[:, 1, :], w_h).then_inc(ld_wx, 16)
            sp.dma_start(misc[0:E * NF, :], b1.rearrange("e (f p) -> (e f) p", p=P)).then_inc(ld_misc, 16)
            sp.dma_start(misc[E * NF:E * NF + 1, :], b_h.rearrange("(a n) -> a n", a=1)).then_inc(ld_misc, 16)
            sp.dma_start(misc[E * NF + 1:NM, :], w_router).then_inc(ld_misc, 16)
            sp.dma_start(b2row[:, :], b2.rearrange("(a e) n -> a (e n)", a=1)).then_inc(ld_b2, 16)
            for i in range(4):
                if i >= 2:
                    sp.wait_ge(nat_done, 4 * (i - 1))
                if i < 2:
                    src = w1[4 * i:4 * i + 4].rearrange("e (f p) h -> p (e f) h", p=P)
                    dst = stage[:, i % 2, :].rearrange("p (n h) -> p n h", h=P)
                else:
                    src = w2[4 * (i - 2):4 * (i - 2) + 4].rearrange("e h f -> h e f")
                    dst = stage[:, i % 2, :].rearrange("p (e f) -> p e f", f=FF)
                sp.dma_start(dst, src).then_inc(ld_stage[i % 2], 16)
            TS = P // B
            out_v = out.rearrange("b (j t) h -> b j t h", t=TS)
            for c in range(CH):
                sp.wait_ge(added, NK + (c + 1) * E * TILES)
                for t in range(TS):
                    sp.dma_start(out_v[:, TILES * c:TILES * (c + 1), t, :],
                                 acc[B * t:B * (t + 1), TILES * c:TILES * (c + 1), :]).then_inc(stored, 16)
            sp.wait_ge(stored, 16 * CH * TS)

        @block.gpsimd
        def _(pool):
            pool_n = [0]

            def link(ins):
                pool_n[0] += 1
                ins.then_inc(pool_step, 1)
                pool.wait_ge(pool_step, pool_n[0])

            link(nc.gpsimd.memset(ident[:, :], 0.0))
            nc.gpsimd.affine_select(out=ident[:, :], in_=ident[:, :], compare_op=ALU.not_equal, fill=1.0, base=0,
                                    pattern=[[-1, P]], channel_multiplier=1).then_inc(consts, 1)
            nc.gpsimd.memset(ones[:, :], 1.0).then_inc(consts, 1)
            nc.gpsimd.memset(ones16[:, :], 1.0).then_inc(consts, 1)
            nc.gpsimd.iota(experts[:, :], [[1, E]], base=0, channel_multiplier=0,
                           allow_small_or_imprecise_dtypes=True).then_inc(consts, 1)
            pool.wait_ge(consts, 4)
            nc.gpsimd.tensor_copy(ident16[:, :], ident[:, :]).then_inc(consts, 1)

            def split(hi, lo, src):
                link(nc.gpsimd.tensor_scalar(src, src, WS, 0.0, ALU.mult, ALU.add))
                link(nc.gpsimd.tensor_scalar(hi, src, 1.0, 0.0, ALU.mult, ALU.add))
                return nc.gpsimd.tensor_tensor(lo, src, hi, ALU.subtract)

            pool.wait_ge(ld_wx, 32)
            split(wxh_hi[:, :, :], wxh_lo[:, :, :], wxh[:, :, :]).then_inc(small_w, 1)
            pool.wait_ge(ld_b2, 16)
            split(b2_hi[:, :, :].rearrange("p e n -> p (e n)"), b2_lo[:, :, :].rearrange("p e n -> p (e n)"),
                  b2row[:, :]).then_inc(small_w, 1)
            for i in range(4):
                pool.wait_ge(ld_stage[i % 2], 16 * (i // 2 + 1))
                for n in range(4):
                    at = 4 * BANK * (i % 2) + BANK * n
                    split(nat[:, 2 * (i // 2), at:at + BANK], nat[:, 2 * (i // 2) + 1, at:at + BANK],
                          stage[:, i % 2, BANK * n:BANK * (n + 1)]).then_inc(nat_done, 1)

        @block.scalar
        def _(act):
            nc.scalar.preload_act_table(ACT.Sqrt)
            act.wait_ge(norm_sb, 1)
            nc.scalar.activation(nrm[:, 1, :], nrm[:, 0, :], ACT.Sqrt).then_inc(root_done, 1)
            nc.scalar.preload_act_table(ACT.Sigmoid)
            for k in range(NK):
                act.wait_ge(xT_mm, k + 1)
                nc.scalar.activation(xT[:, 4 * k:4 * k + 4, :].rearrange("p b t -> p (b t)"), banks[4 + k][:, :],
                                     ACT.Copy).then_inc(xT_sb, 1)
            for n in range(NW):
                act.wait_ge(wT_mm, n + 1)
                nc.scalar.activation(wT_hi[:, n, :], banks[4 + n % WB][:, 0:P], ACT.Copy).then_inc(wT_hi_done, 1)
            act.wait_ge(scale_done, 1)
            for k in range(NK):
                ck = c32[:, 4 * k:4 * k + 4, :].rearrange("p b l -> p (b l)")
                nc.scalar.activation(ck, ck, ACT.Copy, scale=sc[:, 0, 4:5], bias=MAGIC).then_inc(cq_done, 1)
            for k in range(NK):
                act.wait_ge(cT_mm, k + 1)
                nc.scalar.activation(blk(qhi, k), banks[k][:, :], ACT.Copy, bias=-MAGIC).then_inc(q_hi_done, 1)
            for n in range(2 * NJ * NK):
                act.wait_ge(gu_mm, n + 1)
                t, m = (gate2, n) if n < NJ * NK else (up2, n - NJ * NK)
                nc.scalar.activation(blk(t, m), banks[n % GB][:, :], ACT.Copy).then_inc(gu_sb, 1)
            for n in range(NJ):
                act.wait_ge(gateq, n + 1)
                nc.scalar.activation(sig[:, n, :], q16(gate[:, n, :]), ACT.Sigmoid,
                                     scale=sc[:, 1, 2:3]).then_inc(sig_done, 1)
            act.wait_ge(scale_done, 3)
            for n in range(NJ):
                nc.scalar.activation(up[:, n, :], up[:, n, :], ACT.Copy, scale=sc[:, 2, 4:5], bias=MAGIC).then_inc(upq, 1)
            nc.scalar.preload_act_table(ACT.Gelu)
            act.wait_ge(scale_done, 4)
            for n in range(2 * NJ):
                s = sig2[:, n * 1024:(n + 1) * 1024]
                nc.scalar.activation(s, s, ACT.Copy, scale=sc[:, 3, 4:5], bias=MAGIC).then_inc(g2q, 1)
            act.wait_ge(scale_done, 5)
            for k in range(NK):
                for j in range(NJ):
                    n = j * NK + k
                    nc.scalar.activation(blk(up2, n), blk(up2, n), ACT.Copy, scale=sc[:, 4, 4:5],
                                         bias=MAGIC).then_inc(oq, 1)
                    act.wait_ge(oq, NJ * k + j + 1)
                    nc.scalar.activation(blk(o_hi, n), blk(up2, n), ACT.Copy, bias=-MAGIC).then_inc(o_hi_done, 1)
            for k in range(NK):
                act.wait_ge(x1T_mm, k + 1)
                nc.scalar.activation(acc[:, TILES * k:TILES * (k + 1), :].rearrange("p j h -> p (j h)"),
                                     banks[4 + k][:, :], ACT.Copy).then_inc(added, 1)

            act.wait_ge(misc_sb, 1)

            with act.Fori(0, STEPS // 4) as i:
                for j in range(4):
                    act.wait_ge(rnn_mm, i * 4 + (j + 1))
                    z = ps_rnn[j % 2][:, bass.ds(i * 2 * B + (j // 2) * B, B)]
                    nc.scalar.activation(h_hi[:, bass.ds(i * 4 * B + (j + 1) * B, B)], z, ACT.Tanh,
                                         bias=miscT[:, SLOTS:SLOTS + 1], scale=1 / WS).then_inc(h_hi_done, 1)
                    nc.scalar.activation(h32[:, j, :], z, ACT.Tanh,
                                         bias=miscT[:, SLOTS:SLOTS + 1], scale=1 / WS).then_inc(h32_done, 1)

            def pair(c, e2, prev, rnn):
                for s in range(2 * NF):
                    f = s % NF
                    slot = c * SLOTS + e2 * 2 * NF + s
                    if rnn:
                        r = slot + STEPS
                        act.wait_ge(rnn_mm, r + 1)
                        z = ps_rnn[s % 2][:, bass.ds(e2 * NF * B + (s // 2) * B, B)]
                        nc.scalar.activation(h_hi[:, bass.ds(r * B + B, B)], z, ACT.Tanh,
                                             bias=miscT[:, SLOTS:SLOTS + 1], scale=1 / WS).then_inc(h_hi_done, 1)
                        nc.scalar.activation(h32[:, f, :], z, ACT.Tanh,
                                             bias=miscT[:, SLOTS:SLOTS + 1], scale=1 / WS).then_inc(h32_done, 1)
                    bias = miscT[:, bass.ds(e2 * 2 * NF + s, 1)]
                    act.wait_ge(up_mm, slot + 1)
                    if prev or s >= NF:
                        act.wait_ge(g_lo_done, slot - NF + 1)
                    if prev:
                        act.wait_ge(y_mm, slot - 2 * NF + 1)
                    nc.scalar.activation(g32[:, f, :], ps_h[f][:, :], ACT.Gelu, bias=bias, scale=1 / WS).then_inc(g32_done, 1)
                    nc.scalar.activation(g_hi[:, s // NF, f, :], ps_h[f][:, :], ACT.Gelu, bias=bias,
                                         scale=1 / WS).then_inc(g_hi_done, 1)
                    if s == NF + 1:
                        if isinstance(e2, int) and e2 == 0:
                            act.wait_ge(margin_done, c + 1)
                            nc.scalar.activation(mixd[:, 1, :], mixd[:, 0, :], ACT.Tanh, scale=0.5 / WS).then_inc(mix_done, 1)

            chunks(act, pair)

        @block.vector
        def _(dve):
            dve_n = [0]

            def link(ins):
                dve_n[0] += 1
                ins.then_inc(dve_step, 1)
                dve.wait_ge(dve_step, dve_n[0])

            V = nc.vector

            def scales(i, n, unit):
                unit()
                link(V.tensor_scalar(sc[:, i, 1:2], sc[:, i, 0:1], 1.0 / QMAX, None, ALU.mult))
                V.tensor_reduce(pk1[:, i:i + 1], peak[:, i, 0:n], X, ALU.max).then_inc(pk_part, 1)
                dve.wait_ge(pk_row, i + 1)
                V.tensor_reduce(pk0[:, i:i + 1], ps_pk[0:1, 0:P], X, ALU.max).then_inc(pk_one, 1)
                dve.wait_ge(pk_all, i + 1)
                link(V.tensor_scalar(sc[:, i, 2:3], ps_pk[:, P:P + 1], sc[:, i, 1:2], TINY, ALU.mult, ALU.max))
                link(V.reciprocal(sc[:, i, 3:4], sc[:, i, 2:3]))
                V.tensor_scalar(sc[:, i, 4:5], sc[:, i, 3:4], sc[:, i, 0:1], None, ALU.mult).then_inc(scale_done, 1)
                dve.wait_ge(scale_done, i + 1)

            dve.wait_ge(cond_T, 1)
            V.tensor_scalar(wcT[:, :], banks[0][:, 0:P], 1.0 / float(P) ** 0.5, None, ALU.mult).then_inc(cond_sb, 1)
            V.tensor_copy(yT[:, :], banks[0][:, P:P + B]).then_inc(cond_sb, 1)
            dve.wait_ge(cond_sb, 2)
            V.tensor_tensor(wc2[:, :], wcT[:, :], wcT[:, :], ALU.mult).then_inc(norm_in, 1)
            V.tensor_tensor(y2[:, :], yT[:, :], yT[:, :], ALU.mult).then_inc(norm_in, 1)
            for b in range(B):
                V.tensor_scalar(wyT[:, b, :], wcT[:, :], yT[:, b:b + 1], None, ALU.mult).then_inc(wy_done, 1)
            dve.wait_ge(norm_mm, 1)
            V.tensor_scalar(nrm[:, 0, :], banks[1][:, 0:B], 1e-8, None, ALU.add).then_inc(norm_sb, 1)
            link(V.tensor_scalar(h_hi[:, 0:B], yT[:, :], 1.0, None, ALU.mult))
            V.tensor_tensor(h_lo[:, 0:B], yT[:, :], h_hi[:, 0:B], ALU.subtract).then_inc(h_lo_done, 1)
            dve.wait_ge(root_done, 1)
            link(V.reciprocal(nrm[:, 2, :], nrm[:, 1, :]))
            link(V.tensor_tensor(nrm[:, 3, :], nrm[:, 2, :], nrm[:, 2, :], ALU.mult))
            link(V.scalar_tensor_tensor(nrm[:, 4, :], nrm[:, 3, :], -0.5, nrm[:, 0, :], ALU.mult, ALU.mult))
            link(V.tensor_scalar(nrm[:, 3, :], nrm[:, 4, :], 1.5, None, ALU.add))
            link(V.tensor_tensor(nrm[:, 1, :], nrm[:, 3, :], nrm[:, 2, :], ALU.mult))
            dve.wait_ge(ld_w0, 48)
            wb = wn[:, :, :].rearrange("p n (k i) -> p (n k) i", i=WBLK)
            NBLK = NW * P // WBLK

            def per_block(i):
                return ws[:, i, :].unsqueeze(2).to_broadcast([P, NBLK, WBLK])

            link(V.tensor_reduce(ws[:, 0, :], wb, X, ALU.max, apply_absolute_value=True))
            link(V.tensor_scalar(ws[:, 0, :], ws[:, 0, :], 1.0 / 7.0, TINY, ALU.mult, ALU.max))
            link(V.reciprocal(ws[:, 1, :], ws[:, 0, :]))
            link(V.tensor_tensor(wb, wb, per_block(1), ALU.mult))
            link(V.tensor_scalar(wb, wb, MAGIC, MAGIC, ALU.add, ALU.subtract))
            V.scalar_tensor_tensor(wb, wb, WS, per_block(0), ALU.mult, ALU.mult).then_inc(wdeq, 1)
            for k in range(NK):
                dve.wait_ge(c_mm, k + 1)
                V.tensor_tensor(c32[:, 4 * k:4 * k + 4, :], banks[k][:, :].rearrange("p (b l) -> p b l", l=P),
                                nrm[:, 1, 4 * k:4 * k + 4].unsqueeze(2).to_broadcast([P, 4, P]),
                                ALU.mult).then_inc(c_sb, 1)
            for k in range(NK):
                dve.wait_ge(c_sb, k + 1)
                link(V.tensor_reduce(peak[:, 0, k:k + 1], c32[:, 4 * k:4 * k + 4, :].rearrange("p b l -> p (b l)"),
                                     X, ALU.max, apply_absolute_value=True))
            scales(0, NK, lambda: link(V.memset(sc[:, 0, 0:1], 1.0)))
            for n in range(NW):
                dve.wait_ge(wT_hi_done, n + 1)
                V.tensor_tensor(wT_lo[:, n, :], banks[4 + n % WB][:, 0:P], wT_hi[:, n, :],
                                ALU.subtract).then_inc(wT_done, 1)
            for k in range(NK):
                dve.wait_ge(q_hi_done, k + 1)
                V.scalar_tensor_tensor(blk(qlo, k), banks[k][:, :], -MAGIC, blk(qhi, k), ALU.add,
                                       ALU.subtract).then_inc(q_done, 1)
            dve.wait_ge(misc_T, 1)
            V.tensor_copy(miscT[:, :], banks[6][:, 0:NM]).then_inc(misc_sb, 1)
            dve.wait_ge(misc_sb, 1)
            link(V.tensor_scalar(pick[:, 0, 0, :], miscT[:, SLOTS + 1:NM], WS, None, ALU.mult))
            link(V.tensor_scalar(rw_hi[:, :], pick[:, 0, 0, :], 1.0, None, ALU.mult))
            link(V.tensor_tensor(rw_lo[:, :], pick[:, 0, 0, :], rw_hi[:, :], ALU.subtract))
            for n in range(NJ * NK):
                dve.wait_ge(gu_sb, n + 1)
                link(V.tensor_reduce(peak[:, 1, n:n + 1], blk(gate2, n), X, ALU.max, apply_absolute_value=True))
            scales(1, NJ * NK, lambda: link(V.tensor_scalar(sc[:, 1, 0:1], sc[:, 0, 2:3], 1.0 / WS, None, ALU.mult)))
            for n in range(NJ):
                V.tensor_scalar(gate[:, n, :], gate[:, n, :], sc[:, 1, 4:5], MAGIC, ALU.mult, ALU.add).then_inc(gateq, 1)
            for n in range(NJ * NK):
                dve.wait_ge(gu_sb, NJ * NK + n + 1)
                link(V.tensor_reduce(peak[:, 2, n:n + 1], blk(up2, n), X, ALU.max, apply_absolute_value=True))
            scales(2, NJ * NK, lambda: link(V.tensor_scalar(sc[:, 2, 0:1], sc[:, 0, 2:3], 1.0 / WS, None, ALU.mult)))
            for n in range(NJ):
                dve.wait_ge(sig_done, n + 1)
                link(V.tensor_scalar(sig[:, n, :], sig[:, n, :], SIG_MAX, SIG_MAGIC, ALU.min, ALU.add))
                V.tensor_tensor(sig[:, n, :], q16(gate[:, n, :]), q16(sig[:, n, :], U16), ALU.mult).then_inc(g2_done, 1)
                dve.wait_ge(g2_done, n + 1)
                link(V.tensor_reduce(peak[:, 3, n:n + 1], sig[:, n, :], X, ALU.max, apply_absolute_value=True))
            scales(3, NJ, lambda: link(V.tensor_scalar(sc[:, 3, 0:1], sc[:, 1, 2:3], 1.0 / 65536.0, None, ALU.mult)))
            dve.wait_ge(upq, NJ)
            for n in range(2 * NJ):
                dve.wait_ge(g2q, n + 1)
                lo, hi = n * 1024, (n + 1) * 1024
                V.tensor_tensor(up2[:, lo:hi], q16(sig2[:, lo:hi]), q16(up2[:, lo:hi]), ALU.mult).then_inc(p_done, 1)
                dve.wait_ge(p_done, n + 1)
                link(V.tensor_reduce(peak[:, 4, n:n + 1], up2[:, lo:hi], X, ALU.max, apply_absolute_value=True))
            scales(4, 2 * NJ, lambda: link(V.tensor_tensor(sc[:, 4, 0:1], sc[:, 3, 2:3], sc[:, 2, 2:3], ALU.mult)))
            for k in range(NK):
                for j in range(NJ):
                    n = j * NK + k
                    dve.wait_ge(o_hi_done, NJ * k + j + 1)
                    V.scalar_tensor_tensor(blk(o_lo, n), blk(up2, n), -MAGIC, blk(o_hi, n), ALU.add,
                                           ALU.subtract).then_inc(o_done, 1)
            link(V.tensor_scalar(pk1[:, 0:1], sc[:, 4, 2:3], 1.0 / WS, None, ALU.mult))
            for k in range(NK):
                dve.wait_ge(down_mm, k + 1)
                dve.wait_ge(xT_sb, k + 1)
                V.scalar_tensor_tensor(x1[:, :, 4 * k:4 * k + 4].rearrange("p t b -> p b t"),
                                       banks[k][:, :].rearrange("p (b t) -> p b t", t=T), pk1[:, 0:1],
                                       xT[:, 4 * k:4 * k + 4, :], ALU.mult, ALU.add).then_inc(x1_done, 1)
            x1f = x1[:, :, :].rearrange("p t b -> p (t b)")
            dve.wait_ge(x1_done, NK)
            for k in range(NK):
                V.tensor_copy(blk(x1_hi, k), blk(x1f, k)).then_inc(x1_hi_done, 1)
                dve.wait_ge(x1_hi_done, k + 1)
                V.tensor_tensor(blk(x1_lo, k), blk(x1f, k), blk(x1_hi, k), ALU.subtract).then_inc(x1_lo_done, 1)

            with dve.Fori(0, STEPS // 4) as i:
                for j in range(4):
                    dve.wait_ge(h32_done, i * 4 + (j + 1))
                    at = bass.ds(i * 4 * B + (j + 1) * B, B)
                    V.tensor_tensor(h_lo[:, at], h32[:, j, :], h_hi[:, at], ALU.subtract).then_inc(h_lo_done, 1)
                    if j % 2:
                        dve.wait_ge(nat_T, i * 2 + (j // 2 + 1))
                        flat = wt[:, :, :].rearrange("p a n -> p (a n)")
                        V.tensor_copy(flat[:, bass.ds(i * 2048 + (j // 2) * 1024, 1024)],
                                      ps_y[j // 2][:, :].bitcast(F16)).then_inc(wt_done, 1)

            def take_logits(c):
                dve.wait_ge(logits_mm, c + 1)
                V.tensor_copy(logit[:, :, :].rearrange("p j e -> p (j e)"),
                              ps_logits[:, 0:TILES * E]).then_inc(logit_sb, 1)

            def find_top(c):
                for j in range(TILES):
                    V.max(top[:, j, :], logit[:, j, :]).then_inc(top_done, 1)

            def find_experts():
                V.tensor_tensor(mixd[:, 0, :], top[:, :, 0], top[:, :, 1], ALU.subtract).then_inc(margin_done, 1)
                for j in range(TILES):
                    V.max_index(topi[:, j, :], top[:, j, :], logit[:, j, :]).then_inc(top_done, 1)

            def mark_experts():
                for a in range(2):
                    V.tensor_tensor(pick[:, a, :, :], topi[:, :, a:a + 1].to_broadcast([P, TILES, E]),
                                    experts[:, :].unsqueeze(1).to_broadcast([P, TILES, E]),
                                    ALU.is_equal).then_inc(pick_done, 1)

            def mix(c):
                dve.wait_ge(mix_done, c + 1)
                V.tensor_scalar(mixd[:, 2, :], mixd[:, 1, :], 0.5 / WS, 0.5 / WS, ALU.mult, ALU.add).then_inc(pick_done, 1)
                V.tensor_scalar(mixd[:, 3, :], mixd[:, 1, :], -0.5 / WS, 0.5 / WS, ALU.mult, ALU.add).then_inc(pick_done, 1)
                dve.wait_ge(pick_done, 6 * c + 4)
                for a in range(2):
                    V.tensor_tensor(pick[:, a, :, :], pick[:, a, :, :],
                                    mixd[:, 2 + a, :].unsqueeze(2).to_broadcast([P, TILES, E]),
                                    ALU.mult).then_inc(pick_done, 1)
                dve.wait_ge(pick_done, 6 * c + 6)
                V.tensor_tensor(gates[:, bass.ds(c * TILES, TILES), :], pick[:, 0, :, :], pick[:, 1, :, :],
                                ALU.add).then_inc(gates_done, 1)
                dve.wait_ge(gates_done, c + 1)

            def add_gated(c, e, j, par):
                g = gates[:, bass.ds(c * TILES + j, 1), bass.ds(e, 1)].rearrange("p a b -> p (a b)")
                a = acc[:, bass.ds(c * TILES + j, 1), :].rearrange("p a b -> p (a b)")
                V.scalar_tensor_tensor(a, ps_y[par][:, P * j:P * (j + 1)], g, a, ALU.mult, ALU.add).then_inc(added, 1)

            def pair(c, e2, prev, rnn):
                first = isinstance(e2, int) and e2 == 0
                for s in range(2 * NF):
                    f = s % NF
                    slot = c * SLOTS + e2 * 2 * NF + s
                    if rnn:
                        r = slot + STEPS
                        dve.wait_ge(h32_done, r + 1)
                        at = bass.ds(r * B + B, B)
                        V.tensor_tensor(h_lo[:, at], h32[:, f, :], h_hi[:, at], ALU.subtract).then_inc(h_lo_done, 1)
                    if first and s == 1:
                        take_logits(c)
                    if first and s == 2:
                        dve.wait_ge(logit_sb, c + 1)
                    if first and s == 3:
                        dve.wait_ge(top_done, 2 * TILES * c + TILES)
                    if first and s == 4:
                        dve.wait_ge(top_done, 2 * TILES * (c + 1))
                    if first and s == 6:
                        mix(c)
                    dve.wait_ge(g_hi_done, slot + 1)
                    if prev:
                        dve.wait_ge(y_mm, slot - 2 * NF + 1)
                    V.tensor_tensor(g_lo[:, s // NF, f, :], g32[:, f, :], g_hi[:, s // NF, f, :],
                                    ALU.subtract).then_inc(g_lo_done, 1)
                    if first and s == 2:
                        find_top(c)
                    if first and s == 3:
                        find_experts()
                    if first and s == 4:
                        mark_experts()
                    if prev:
                        cc, e = (c - 1, E - 2 + s // NF) if first else (c, e2 * 2 - 2 + s // NF)
                        dve.wait_ge(y_mm, slot - f - NF)
                        dve.wait_ge(added, NK + slot - 2 * NF - f)
                        add_gated(cc, e, f, s // NF)

            chunks(dve, pair)
            for s in range(2 * NF):
                if s % NF == 0:
                    dve.wait_ge(y_mm, CH * SLOTS - NF + s)
                    dve.wait_ge(added, NK + CH * SLOTS - 2 * NF + s)
                add_gated(CH - 1, E - 2 + s // NF, s % NF, s // NF)

        @block.tensor
        def _(pe):
            def mm(o, l, r, start, stop=True):
                return nc.tensor.matmul(o, l, r, start=start, stop=stop, skip_group_check=True)

            def mm3(o, l_hi, l_lo, r_hi, r_lo, start=True):
                mm(o, l_hi, r_hi, start)
                mm(o, l_lo, r_hi, False)
                return mm(o, l_hi, r_lo, False)

            def spread_peak(i):
                pe.wait_ge(pk_part, i + 1)
                nc.tensor.transpose(ps_pk[0:1, 0:P], pk1[:, i:i + 1], ident[:, :]).then_inc(pk_row, 1)
                pe.wait_ge(pk_one, i + 1)
                mm(ps_pk[:, P:P + 1], ones[:, :], pk0[:, i:i + 1], True).then_inc(pk_all, 1)

            pe.wait_ge(consts, 5)
            pe.wait_ge(ld_cond, 32)
            nc.tensor.transpose(banks[0][:, 0:P], wc[:, :], ident[:, :])
            nc.tensor.transpose(banks[0][:, P:P + B], y_sb[:, :], ident[0:B, 0:B]).then_inc(cond_T, 1)
            pe.wait_ge(norm_in, 2)
            mm(banks[1][:, 0:B], wc2[:, :], y2[:, :], True).then_inc(norm_mm, 1)
            for b in range(B):
                pe.wait_ge(ld_x, 32)
                last = nc.tensor.transpose(banks[4 + b // 4][:, P * (b % 4):P * (b % 4 + 1)], x_sb[:, b, :], ident[:, :])
                if b % 4 == 3:
                    last.then_inc(xT_mm, 1)
            pe.wait_ge(norm_sb, 1)
            for b in range(B):
                pe.wait_ge(wy_done, b + 1)
                last = mm(banks[b // 4][:, P * (b % 4):P * (b % 4 + 1)], wyT[:, b, :], x_sb[:, b, :], True)
                if b % 4 == 3:
                    last.then_inc(c_mm, 1)
            pe.wait_ge(wdeq, 1)
            pe.wait_ge(xT_sb, NK)
            for n in range(WB):
                nc.tensor.transpose(banks[4 + n][:, 0:P], wn[:, n, :], ident[:, :]).then_inc(wT_mm, 1)
            spread_peak(0)
            for n in range(WB, NW):
                pe.wait_ge(wT_done, n - WB + 1)
                nc.tensor.transpose(banks[4 + n % WB][:, 0:P], wn[:, n, :], ident[:, :]).then_inc(wT_mm, 1)
            for k in range(NK):
                pe.wait_ge(cq_done, k + 1)
                for b in range(4 * k, 4 * k + 4):
                    last = nc.tensor.transpose(banks[k][:, P * (b % 4):P * (b % 4 + 1)], c32[:, b, :], ident[:, :])
                last.then_inc(cT_mm, 1)
            pe.wait_ge(ld_misc, 48)
            pe.wait_ge(wT_done, NW)
            nc.tensor.transpose(banks[6][:, 0:NM], misc[:, :], ident[0:NM, 0:NM]).then_inc(misc_T, 1)
            pe.wait_ge(q_done, NK)
            for n in range(2 * NJ * NK):
                j, k = n // NK, n % NK
                if n >= GB:
                    pe.wait_ge(gu_sb, n - GB + 1)
                if n == NJ * NK + 6:
                    spread_peak(1)
                mm3(banks[n % GB][:, :], wT_hi[:, j, :], wT_lo[:, j, :], blk(qhi, k), blk(qlo, k)).then_inc(gu_mm, 1)
            for i in range(2, 5):
                spread_peak(i)
            for k in range(NK):
                pe.wait_ge(o_done, NJ * (k + 1))
                for j in range(NJ):
                    n = j * NK + k
                    last = mm3(banks[k][:, :], wT_hi[:, 2 * NJ + j, :], wT_lo[:, 2 * NJ + j, :], blk(o_hi, n), blk(o_lo, n), j == 0)
                last.then_inc(down_mm, 1)
            x1f = x1[:, :, :].rearrange("p t b -> p (t b)")
            pe.wait_ge(x1_done, NK)
            for j in range(CH * TILES):
                last = nc.tensor.transpose(banks[4 + j // 4][:, P * (j % 4):P * (j % 4 + 1)], x1f[:, P * j:P * (j + 1)], ident[:, :])
                if j % 4 == 3:
                    last.then_inc(x1T_mm, 1)

            def input_part(c):
                for a in range(2):
                    hi, lo = (t[:, bass.ds(c * BANK, BANK)].rearrange("p (t a b) -> p t a b", a=2, b=B)[:, :, a, :]
                              for t in (x1_hi, x1_lo))
                    mm3(ps_rnn[a][:, 0:BANK // 2].rearrange("p (t b) -> p t b", b=B), wxh_hi[:, 0, :], wxh_lo[:, 0, :], hi, lo)

            def step(r, z):
                h = bass.ds(r * B, B)
                mm(z, wxh_hi[:, 1, :], h_hi[:, h], False)
                mm(z, wxh_lo[:, 1, :], h_hi[:, h], False)
                pe.wait_ge(h_lo_done, r + 1)
                mm(z, wxh_hi[:, 1, :], h_lo[:, h], False).then_inc(rnn_mm, 1)

            pe.wait_ge(small_w, 2)
            pe.wait_ge(x1_lo_done, NK)
            pe.wait_ge(nat_done, 16)
            input_part(0)
            natf = nat[:, :, :].rearrange("p a n -> p (a n)")
            with pe.Fori(0, STEPS // 4) as i:
                for j in range(4):
                    if j:
                        pe.wait_ge(h_hi_done, i * 4 + j)
                    step(i * 4 + j, ps_rnn[j % 2][:, bass.ds(i * 2 * B + (j // 2) * B, B)])
                    if j % 2:
                        for n in range(8):
                            last = nc.tensor.transpose(ps_y[j // 2][:, :].bitcast(F16)[:, P * n:P * (n + 1)],
                                                       natf[:, bass.ds(i * 2048 + (j // 2) * 1024 + P * n, P)], ident16[:, :])
                        last.then_inc(nat_T, 1)
                pe.wait_ge(wt_done, i * 2 + 2)
                pe.wait_ge(h_hi_done, i * 4 + 4)
            pe.wait_ge(added, NK)

            def logits(c):
                for j in range(TILES):
                    t = bass.ds(c * BANK + (P * j + B), P)
                    o = ps_logits[:, E * j:E * (j + 1)]
                    mm(o, h_hi[:, t], rw_hi[:, :], j == 0)
                    mm(o, h_hi[:, t], rw_lo[:, :], False)
                    mm(o, h_lo[:, t], rw_hi[:, :], False)
                    last = mm(o, h_lo[:, t], rw_lo[:, :], False)
                last.then_inc(logits_mm, 1)

            def start_y(e, par):
                rows = lambda t: t[:, bass.ds(e, 1), :].to_broadcast([1, TILES, P])
                y = ps_y[par][:, :].rearrange("p (j h) -> p j h", h=P)
                mm(y, ones16[:, :], rows(b2_hi), True)
                mm(y, ones16[:, :], rows(b2_lo), False)

            def down(e, par, f):
                w = bass.ds(e * FF + f * P, P)
                for j in range(TILES):
                    o = ps_y[par][:, P * j:P * (j + 1)]
                    tile = slice(P * j, P * (j + 1))
                    mm(o, g_hi[:, par, f, tile], w2T_hi[:, w], False)
                    mm(o, g_hi[:, par, f, tile], w2T_lo[:, w], False)
                    last = mm(o, g_lo[:, par, f, tile], w2T_hi[:, w], False)
                last.then_inc(y_mm, 1)

            def pair(c, e2, prev, rnn):
                first = isinstance(e2, int) and e2 == 0
                for s in range(2 * NF):
                    f, par = s % NF, s // NF
                    slot = c * SLOTS + e2 * 2 * NF + s
                    if first and s == 0:
                        pe.wait_ge(h_lo_done, (c + 1) * STEPS + 1)
                        pe.wait_ge(h_hi_done, (c + 1) * STEPS)
                        if rnn:
                            input_part(c + 1)
                    if rnn:
                        r = slot + STEPS
                        pe.wait_ge(h_hi_done, r)
                        step(r, ps_rnn[s % 2][:, bass.ds(e2 * NF * B + (s // 2) * B, B)])
                    if prev or s >= NF:
                        pe.wait_ge(g_hi_done, slot - NF + 1)
                    if first and s == NF - 1:
                        pe.wait_ge(logit_sb, c + 1)
                    w = bass.ds(e2 * 2 * FF + s * P, P)
                    t = bass.ds(c * BANK + B, BANK)
                    mm3(ps_h[f][:, :], w1T_hi[:, w], w1T_lo[:, w], h_hi[:, t], h_lo[:, t]).then_inc(up_mm, 1)
                    if first and s == 1:
                        if prev:
                            pe.wait_ge(g_hi_done, slot - 1)
                        logits(c)
                    if prev or s >= NF:
                        e = e2 * 2 + par - 1 if not first else (E - 1 if par == 0 else 0)
                        if f == 0:
                            if prev:
                                pe.wait_ge(added, NK + slot - 2 * NF)
                            start_y(e, 1 - par)
                        pe.wait_ge(g_lo_done, slot - NF + 1)
                        down(e, 1 - par, f)

            chunks(pe, pair)
            for f in range(NF):
                if f == 0:
                    pe.wait_ge(added, NK + CH * SLOTS - 2 * NF)
                    start_y(E - 1, 1)
                pe.wait_ge(g_lo_done, CH * SLOTS - NF + f + 1)
                down(E - 1, 1, f)


def kernel(x, cond_1024, L0_cond_weight, L0_ffn_w_gate, L0_ffn_w_up, L0_ffn_w_down, L1_cond_Wx, L1_cond_Wh, L1_cond_b,
           L1_ffn_router_w, L1_ffn_w1, L1_ffn_b1, L1_ffn_w2, L1_ffn_b2):
    import numpy as np
    import concourse.bacc as bacc
    from concourse.bass_utils import run_bass_kernel_spmd

    nc = bacc.Bacc("TRN2", target_bir_lowering=False, num_devices=1)
    given = {"x": x, "cond": cond_1024, "w_cond": L0_cond_weight, "w_gate": L0_ffn_w_gate, "w_up": L0_ffn_w_up,
             "w_down": L0_ffn_w_down, "w_x": L1_cond_Wx, "w_h": L1_cond_Wh, "b_h": L1_cond_b,
             "w_router": L1_ffn_router_w, "w1": L1_ffn_w1, "b1": L1_ffn_b1, "w2": L1_ffn_w2, "b2": L1_ffn_b2}
    arrays = {f"in_{n}": np.ascontiguousarray(a) for n, a in given.items()}
    aps = [nc.dram_tensor(n, a.shape, mybir.dt.from_np(a.dtype), kind="ExternalInput").ap() for n, a in arrays.items()]
    out = nc.dram_tensor("out_block", x.shape, F32, kind="ExternalOutput").ap()
    program(nc, *aps, out)
    r = run_bass_kernel_spmd(nc, [arrays], core_ids=[0])
    return r.results[0]["out_block"]
```

```python
from contextlib import ExitStack

import concourse.bass as bass
from concourse import mybir

F32, F16 = mybir.dt.float32, mybir.dt.float16
I8, U8 = mybir.dt.int8, mybir.dt.uint8
I16, U16 = mybir.dt.int16, mybir.dt.uint16
ALU = mybir.AluOpType
ACT = mybir.ActivationFunctionType
X, XY = mybir.AxisListType.X, mybir.AxisListType.XY

P = 128
B = 16
T = 128
TOK = B * T
INNER = 384
NJ = INNER // P
BANK = 512
NK = TOK // BANK
WBLK = 32
NW = 3 * NJ
E, FF = 8, 512
NF = FF // P
CT = 512
STEPS = CT // B
CH = T // STEPS
TILES = CT // P
TS = P // B
SLOTS = E * NF
WS = 256.0
QMAX = 32767.0
TINY = 1e-12
MAGIC = 12582912.0
SIG_MAGIC = 192.0
SIG_MAX = 65535.0 / 65536.0
EARLY_STEPS = 8
PIECE = E * NF * P // 4
GROUPS = 4 * E * NF // 8
GROUPS_BY = (5, 5, 5, 6, 7, 8, 10)
WY_V = 10


def program(nc, x, cond, w_cond, w_gate, w_up, w_down, w_x, w_h, b_h, w_router, w1, b1, w2, b2, out):
    ctx = ExitStack()
    with ctx:
        def sb(name, shape, dt=F32):
            return ctx.enter_context(nc.sbuf_tensor(name, shape, dt))

        def sem(name):
            return ctx.enter_context(nc.semaphore(name))

        def sems(names):
            return [sem(n) for n in names.split()]

        banks = [ctx.enter_context(nc.psum_tensor(f"bank{i}", [P, BANK], F32)) for i in range(8)]

        ident = sb("ident", [P, P])
        ident16 = sb("ident16", [P, P], F16)
        ones2 = sb("ones2", [2, P], F16)
        experts = sb("experts", [P, E])
        x_sb = sb("x_sb", [P, B, P])
        xT = sb("xT", [P, TOK])
        wc = sb("wc", [P, P])
        y_sb = sb("y_sb", [B, P])
        wcT = sb("wcT", [P, P])
        yT = sb("yT", [P, B])
        wc2 = sb("wc2", [P, P])
        y2 = sb("y2", [P, B])
        nrm = sb("nrm", [P, 5, B])
        wyT = sb("wyT", [P, B, P])
        c32 = sb("c32", [P, B, P])
        q = sb("q", [P, 2, TOK], F16)
        qhi, qlo = q[:, 0, :], q[:, 1, :]
        wn = sb("wn", [P, NW, P])
        ws = sb("ws", [P, 3, NW * P // WBLK])
        wT_hi = sb("wT_hi", [P, NW, P], F16)
        wT_lo = sb("wT_lo", [P, NW, P], F16)
        big = sb("big", [P, 3 * NJ * TOK])
        gate2, up2, sig2 = (big[:, i * NJ * TOK:(i + 1) * NJ * TOK] for i in range(3))
        peak = sb("peak", [P, 5, NJ * NK])
        pk1 = sb("pk1", [P, 5])
        pkm = sb("pkm", [P, 5])
        sc = sb("sc", [P, 5, 5])
        x1 = c32[:, :, :].rearrange("p b l -> p (b l)")
        x1_hi, x1_lo = (x_sb[:, :, :].rearrange("p b l -> p (b l)").bitcast(F16)[:, i * TOK:(i + 1) * TOK] for i in range(2))
        acc = wyT
        h32 = q[:, :, :].rearrange("p a n -> p (a n)").bitcast(F32)
        wxh = sb("wxh", [P, 2, P])
        wx_hi = sb("wx_hi", [P, P], F16)
        wx_lo = sb("wx_lo", [P, P], F16)
        NM = E * NF + 1 + E
        misc = sb("misc", [NM, P])
        miscT = sb("miscT", [P, NM])
        rw = sb("rw", [P, E])
        rw_hi = sb("rw_hi", [P, E], F16)
        rw_lo = sb("rw_lo", [P, E], F16)
        b2lo = sb("b2lo", [1, E * P], F16)
        b2s = sb("b2s", [2, E, P], F16)
        stage = sb("stage", [P, 2, PIECE])
        nat = sb("nat", [P, 4 * SLOTS * P], F16)
        wt = sb("wt", [P, 4 * SLOTS * P], F16)
        b2row = wt[:, :].bitcast(F32)[0:1, 0:E * P]
        g32 = sig2[:, 0:NF * CT].rearrange("p (f n) -> p f n", f=NF)
        g_hi, g_lo = (sig2.bitcast(F16)[:, 2 * NF * CT * (i + 1):2 * NF * CT * (i + 2)].rearrange("p (a f n) -> p a f n", a=2, f=NF)
                      for i in range(2))
        h_hi, h_lo = (up2.bitcast(F16)[:, TOK * i:TOK * (i + 1)] for i in range(2))
        logit = sb("logit", [P, TILES, E])
        top = sb("top", [P, TILES, 8])
        topi = sb("topi", [P, TILES, 8], U16)
        mixd = sb("mixd", [P, 4, TILES])
        pick = sb("pick", [P, 2, TILES, E])
        gates = sb("gates", [P, CH * TILES, E])

        ld_x = [sem(f"ld_x{i}") for i in range(4)]
        ld_cond, ld_w0, ld_misc, ld_wx, ld_b2, ld_stage0, ld_stage1 = sems(
            "ld_cond ld_w0 ld_misc ld_wx ld_b2 ld_stage0 ld_stage1")
        ld_stage = [ld_stage0, ld_stage1]
        consts, cond_T, cond_sb, norm_in, norm_mm, norm_sb, root_done = sems(
            "consts cond_T cond_sb norm_in norm_mm norm_sb root_done")
        xT_mm, xT_sb, wy_v, wy_s, c_mm, c_sb, cT_mm, cq_done, q_hi_v, q_hi_s, q_done = sems(
            "xT_mm xT_sb wy_v wy_s c_mm c_sb cT_mm cq_done q_hi_v q_hi_s q_done")
        w_scales, wdeq, wT_mm, wT_hi_done, wT_done, misc_T, misc_sb = sems(
            "w_scales wdeq wT_mm wT_hi_done wT_done misc_T misc_sb")
        pk_part, pk_all, scale_done, dve_step, pool_step = sems("pk_part pk_all scale_done dve_step pool_step")
        gu_mm, gu_sb, gateq, upq, sig_done, g2_done, p_pool, g2q, p_done, oq, o_hi_done, o_lo_done = sems(
            "gu_mm gu_sb gateq upq sig_done g2_done p_pool g2q p_done oq o_hi_done o_lo_done")
        down_mm, x1_done, x1_hi_done, x1_lo_done, x1T_mm = sems("down_mm x1_done x1_hi_done x1_lo_done x1T_mm")
        nat_done, small_w, b2_moved, nat_T, wt_done = sems("nat_done small_w b2_moved nat_T wt_done")
        rnn_mm, h32_done, h_hi_done, h_lo_done = sems("rnn_mm h32_done h_hi_done h_lo_done")
        logits_mm, logit_sb, top_done, margin_done, mix_done, pick_done, gates_done = sems(
            "logits_mm logit_sb top_done margin_done mix_done pick_done gates_done")
        hid_mm, g32_done, g_hi_done, hi_v, g_lo_done, y_mm, added, stored = sems(
            "hid_mm g32_done g_hi_done hi_v g_lo_done y_mm added stored")

        ps_rnn = banks[0]
        ps_y = [banks[1], banks[2]]
        ps_logits = banks[3]
        ps_h = banks[4:8]
        ps_pk = banks[7]
        Q_HI_SCALAR = (2, 3)
        GU_BANKS = [4, 5, 6, 0, 1, 2]
        w1T_hi, w1T_lo, w2T_hi, w2T_lo = (wt[:, i * SLOTS * P:(i + 1) * SLOTS * P] for i in range(4))

        def q16(t, dt=I16):
            return t.bitcast(dt)[:, 0::2]

        def blk(t, n):
            return t[:, BANK * n:BANK * (n + 1)]

        def third(t, n):
            return t[:, TOK * n:TOK * (n + 1)]

        def sixth(t, n):
            return t[:, TOK // 2 * n:TOK // 2 * (n + 1)]

        def tokens(t, k):
            return t.rearrange("p (j n) -> p j n", j=NJ)[:, :, BANK * k:BANK * (k + 1)]

        def time_major(t, k):
            return t.rearrange("p (t b) -> p b t", b=B)[:, 4 * k:4 * k + 4, :]

        def batches(t):
            return t.rearrange("p (b n) -> p b n", n=P)

        o_hi = gate2.bitcast(F16)[:, 0:NJ * TOK]
        o_lo = gate2.bitcast(F16)[:, NJ * TOK:2 * NJ * TOK]

        def chunks(eng, pair):
            def chunk(c, prev, rnn):
                pair(c, 0, prev, rnn)
                with eng.Fori(1, E // 2) as e2:
                    pair(c, e2, True, rnn)
            chunk(0, False, True)
            with eng.Fori(1, CH - 1) as c:
                chunk(c, True, True)
            chunk(CH - 1, True, False)

        block = ctx.enter_context(nc.Block())

        @block.sync
        def _(sp):
            sp.dma_start(wc[:, :], w_cond.rearrange("a o i c -> (a o) (i c)")).then_inc(ld_cond, 16)
            sp.dma_start(y_sb[:, :], cond).then_inc(ld_cond, 16)
            for h in range(4):
                sp.dma_start(x_sb[:, 4 * h:4 * h + 4, :],
                             x[4 * h:4 * h + 4].rearrange("b p l -> p b l")).then_inc(ld_x[h], 16)
            sp.dma_start(wn[:, 0:NJ, :], w_gate.rearrange("(j p) i -> p j i", p=P)).then_inc(ld_w0, 16)
            sp.dma_start(wn[:, NJ:2 * NJ, :], w_up.rearrange("(j p) i -> p j i", p=P)).then_inc(ld_w0, 16)
            sp.dma_start(wn[:, 2 * NJ:NW, :], w_down.rearrange("p (j i) -> p j i", j=NJ)).then_inc(ld_w0, 16)
            sp.dma_start(wxh[:, 0, :], w_x).then_inc(ld_wx, 16)
            sp.dma_start(wxh[:, 1, :], w_h).then_inc(ld_wx, 16)
            sp.dma_start(misc[0:E * NF, :], b1.rearrange("e (f p) -> (e f) p", p=P)).then_inc(ld_misc, 16)
            sp.dma_start(misc[E * NF:E * NF + 1, :], b_h.rearrange("(a n) -> a n", a=1)).then_inc(ld_misc, 16)
            sp.dma_start(misc[E * NF + 1:NM, :], w_router).then_inc(ld_misc, 16)
            sp.dma_start(b2row, b2.rearrange("(a e) n -> a (e n)", a=1)).then_inc(ld_b2, 16)
            for i in range(8):
                if i >= 2:
                    sp.wait_ge(nat_done, 2 * (i - 1))
                if i < 4:
                    src = w1[2 * i:2 * i + 2].rearrange("e (f p) h -> p (e f) h", p=P)
                    dst = stage[:, i % 2, :].rearrange("p (n h) -> p n h", h=P)
                else:
                    src = w2[2 * (i - 4):2 * (i - 4) + 2].rearrange("e h f -> h e f")
                    dst = stage[:, i % 2, :].rearrange("p (e f) -> p e f", f=FF)
                sp.dma_start(dst, src).then_inc(ld_stage[i % 2], 16)
                if i == 1:
                    sp.wait_ge(small_w, 2)
                    sp.dma_start(b2s[1:2, :, :].rearrange("p e n -> p (e n)"), b2lo[:, :]).then_inc(b2_moved, 16)
            out_v = out.rearrange("b (j t) h -> b j t h", t=TS)
            for c in range(CH):
                sp.wait_ge(added, NK + (c + 1) * E * TILES)
                for t in range(TS):
                    sp.dma_start(out_v[:, TILES * c:TILES * (c + 1), t, :],
                                 acc[B * t:B * (t + 1), TILES * c:TILES * (c + 1), :]).then_inc(stored, 16)
            sp.wait_ge(stored, 16 * CH * TS)

        @block.gpsimd
        def _(pool):
            pool_n = [0]

            def link(ins):
                pool_n[0] += 1
                ins.then_inc(pool_step, 1)
                pool.wait_ge(pool_step, pool_n[0])

            G = nc.gpsimd
            link(G.memset(ident[:, :], 0.0))
            G.affine_select(out=ident[:, :], in_=ident[:, :], compare_op=ALU.not_equal, fill=1.0, base=0,
                            pattern=[[-1, P]], channel_multiplier=1).then_inc(consts, 1)
            G.memset(ones2[:, :], 1.0).then_inc(consts, 1)
            G.iota(experts[:, :], [[1, E]], base=0, channel_multiplier=0,
                   allow_small_or_imprecise_dtypes=True).then_inc(consts, 1)
            pool.wait_ge(consts, 3)
            G.tensor_copy(ident16[:, :], ident[:, :]).then_inc(consts, 1)

            def split(hi, lo, src):
                link(G.tensor_scalar(src, src, WS, 0.0, ALU.mult, ALU.add))
                link(G.tensor_scalar(hi, src, 1.0, 0.0, ALU.mult, ALU.add))
                return G.tensor_tensor(lo, src, hi, ALU.subtract)

            pool.wait_ge(ld_wx, 32)
            split(wx_hi[:, :], wx_lo[:, :], wxh[:, 0, :]).then_inc(small_w, 1)
            link(G.tensor_scalar(wxh[:, 1, :], wxh[:, 1, :], WS, 0.0, ALU.mult, ALU.add))
            pool.wait_ge(w_scales, 1)
            wb = wn[:, :, :].rearrange("p n (k i) -> p (n k) i", i=WBLK)

            def per_block(i):
                return ws[:, i, :].unsqueeze(2).to_broadcast([P, NW * P // WBLK, WBLK])

            link(G.tensor_tensor(wb, wb, per_block(1), ALU.mult))
            link(G.tensor_scalar(wb, wb, 1.0, MAGIC, ALU.mult, ALU.add))
            link(G.tensor_scalar(wb, wb, 1.0, -MAGIC, ALU.mult, ALU.add))
            G.tensor_tensor(wb, wb, per_block(2), ALU.mult).then_inc(wdeq, 1)
            pool.wait_ge(ld_b2, 16)
            split(b2s[0:1, :, :].rearrange("p e n -> p (e n)"), b2lo[:, :], b2row).then_inc(small_w, 1)
            for i in range(8):
                pool.wait_ge(ld_stage[i % 2], 16 * (i // 2 + 1))
                for n in range(PIECE // BANK):
                    at = 2 * (i // 4) * SLOTS * P + PIECE * (i % 4) + BANK * n
                    split(nat[:, at:at + BANK], nat[:, at + SLOTS * P:at + SLOTS * P + BANK],
                          stage[:, i % 2, BANK * n:BANK * (n + 1)]).then_inc(nat_done, 1)
            pool.wait_ge(upq, NJ)
            for n in (1, 4):
                link(G.tensor_scalar(sixth(up2, n), sixth(up2, n), 1.0, -MAGIC, ALU.mult, ALU.add))
            for n in (1, 4):
                pool.wait_ge(g2q, n + 1)
                link(G.tensor_scalar(sixth(sig2, n), sixth(sig2, n), 1.0, -MAGIC, ALU.mult, ALU.add))
                G.tensor_tensor(sixth(up2, n), sixth(sig2, n), sixth(up2, n), ALU.mult).then_inc(p_pool, 1)
            pool.wait_ge(o_hi_done, NK)
            pool.wait_ge(o_lo_done, NK)
            with pool.Fori(0, T // 4) as i:
                pool.wait_ge(h32_done, i * 4 + 4)
                at = bass.ds(i * 4 * B, 4 * B)
                G.tensor_copy(h_hi[:, at], h32[:, at]).then_inc(h_hi_done, 1)
                pool.wait_ge(h_hi_done, i + 1)
                at = bass.ds(i * 4 * B, 4 * B)
                G.tensor_tensor(h_lo[:, at], h32[:, at], h_hi[:, at], ALU.subtract).then_inc(h_lo_done, 1)

        @block.scalar
        def _(act):
            A = nc.scalar.activation

            def take_group(n):
                act.wait_ge(nat_T, n + 1)
                A(wt[:, 1024 * n:1024 * (n + 1)], banks[4 + n % 2][:, :].bitcast(F16), ACT.Copy).then_inc(wt_done, 1)

            nc.scalar.preload_act_table(ACT.Sqrt)
            act.wait_ge(cond_sb, 2)
            for b in range(WY_V, B):
                A(wyT[:, b, :], wcT[:, :], ACT.Copy, scale=yT[:, b:b + 1]).then_inc(wy_s, 1)
            act.wait_ge(norm_sb, 1)
            A(nrm[:, 1, :], nrm[:, 0, :], ACT.Sqrt).then_inc(root_done, 1)
            nc.scalar.preload_act_table(ACT.Sigmoid)
            for k in range(NK):
                act.wait_ge(xT_mm, k + 1)
                A(time_major(xT[:, :], k), batches(banks[4 + k][:, :]), ACT.Copy).then_inc(xT_sb, 1)
            act.wait_ge(scale_done, 1)
            def take_weights(n):
                act.wait_ge(wT_mm, n + 1)
                A(wT_hi[:, NJ * n:NJ * (n + 1), :].rearrange("p j o -> p (j o)"), banks[4 + n][:, 0:NJ * P],
                  ACT.Copy).then_inc(wT_hi_done, 1)

            for k in range(NK):
                act.wait_ge(cT_mm, k + 1)
                A(c32[:, 4 * k:4 * k + 4, :].rearrange("p b l -> p (b l)"), banks[k][:, :], ACT.Copy,
                  scale=sc[:, 0, 4:5], bias=MAGIC).then_inc(cq_done, 1)
                if k == 1:
                    take_weights(0)
            take_weights(1)
            take_weights(2)
            for i, k in enumerate(Q_HI_SCALAR):
                act.wait_ge(cq_done, NK)
                A(time_major(qhi, k), c32[:, 4 * k:4 * k + 4, :], ACT.Copy, bias=-MAGIC).then_inc(q_hi_s, 1)
            for n in range(2 * NJ * NK):
                act.wait_ge(gu_mm, n + 1)
                t, k, j = (gate2, up2)[n // (NJ * NK)], n % (NJ * NK) // NJ, n % NJ
                A(blk(t, j * NK + k), banks[GU_BANKS[n % 6]][:, :], ACT.Copy).then_inc(gu_sb, 1)
            act.wait_ge(scale_done, 2)
            for n in range(NJ):
                A(third(gate2, n), third(gate2, n), ACT.Copy, scale=sc[:, 1, 4:5], bias=MAGIC).then_inc(gateq, 1)
                act.wait_ge(gateq, n + 1)
                A(third(sig2, n), q16(third(gate2, n)), ACT.Sigmoid, scale=sc[:, 1, 2:3]).then_inc(sig_done, 1)
            act.wait_ge(scale_done, 3)
            for n in range(NJ):
                A(third(up2, n), third(up2, n), ACT.Copy, scale=sc[:, 2, 4:5], bias=MAGIC).then_inc(upq, 1)
            nc.scalar.preload_act_table(ACT.Gelu)
            for n in range(GROUPS_BY[0]):
                take_group(n)
            act.wait_ge(scale_done, 4)
            for n in range(2 * NJ):
                A(sixth(sig2, n), sixth(sig2, n), ACT.Copy, scale=sc[:, 3, 4:5], bias=MAGIC).then_inc(g2q, 1)
                for m in range(GROUPS_BY[n], GROUPS_BY[n + 1]):
                    take_group(m)
            for k in range(NK):
                act.wait_ge(oq, k + 1)
                A(tokens(o_lo, k), tokens(up2.bitcast(U8)[:, 0::4], k), ACT.Copy).then_inc(o_lo_done, 1)
            act.wait_ge(misc_sb, 1)
            bias_h = miscT[:, SLOTS:SLOTS + 1]

            def first_step(r):
                act.wait_ge(rnn_mm, r + 1)
                at = slice(r * B, (r + 1) * B)
                A(h32[:, at], ps_rnn[:, at], ACT.Tanh, bias=bias_h, scale=1 / WS).then_inc(h32_done, 1)

            for r in range(EARLY_STEPS - 1):
                first_step(r)
            for k in range(NK):
                if k == NK // 2:
                    first_step(EARLY_STEPS - 1)
                act.wait_ge(x1T_mm, k + 1)
                A(acc[:, 4 * k:4 * k + 4, :].rearrange("p j h -> p (j h)"), banks[4 + k][:, :], ACT.Copy).then_inc(added, 1)
            for r in range(EARLY_STEPS, STEPS):
                first_step(r)

            def pair(c, e2, prev, rnn):
                first = isinstance(e2, int)
                for s in range(2 * NF):
                    f = s % NF
                    slot = c * SLOTS + e2 * 2 * NF + s
                    if rnn:
                        act.wait_ge(rnn_mm, slot + (STEPS + 1))
                        A(h32[:, bass.ds((slot + STEPS) * B, B)], ps_rnn[:, bass.ds(e2 * 2 * NF * B + s * B, B)], ACT.Tanh,
                          bias=bias_h, scale=1 / WS).then_inc(h32_done, 1)
                    act.wait_ge(hid_mm, slot + 1)
                    bias = miscT[:, bass.ds(e2 * 2 * NF + s, 1)]
                    A(g32[:, f, :], ps_h[f][:, 0:CT], ACT.Gelu, bias=bias, scale=1 / WS).then_inc(g32_done, 1)
                    if f % 2:
                        A(g_hi[:, s // NF, f, :], ps_h[f][:, 0:CT], ACT.Gelu, bias=bias, scale=1 / WS).then_inc(g_hi_done, 1)
                    if first and s == NF + 1:
                        act.wait_ge(margin_done, c + 1)
                        A(mixd[:, 1, :], mixd[:, 0, :], ACT.Tanh, scale=0.5 / WS).then_inc(mix_done, 1)

            chunks(act, pair)

        @block.vector
        def _(dve):
            dve_n = [0]

            def link(ins):
                dve_n[0] += 1
                ins.then_inc(dve_step, 1)
                dve.wait_ge(dve_step, dve_n[0])

            V = nc.vector

            def peak_to_scale(i, n, unit):
                V.tensor_reduce(pk1[:, i:i + 1], peak[:, i, 0:n], X, ALU.max).then_inc(pk_part, 1)
                unit(sc[:, i, 0:1])
                link(V.tensor_scalar(sc[:, i, 1:2], sc[:, i, 0:1], 1.0 / QMAX, None, ALU.mult))
                dve.wait_ge(pk_all, i + 1)
                link(V.tensor_reduce(pkm[:, i:i + 1], ps_pk[:, 0:P], X, ALU.max))
                link(V.tensor_scalar(sc[:, i, 2:3], pkm[:, i:i + 1], sc[:, i, 1:2], TINY, ALU.mult, ALU.max))
                link(V.reciprocal(sc[:, i, 3:4], sc[:, i, 2:3]))
                V.tensor_scalar(sc[:, i, 4:5], sc[:, i, 3:4], sc[:, i, 0:1], None, ALU.mult).then_inc(scale_done, 1)
                dve.wait_ge(scale_done, i + 1)

            def block_peak(i, n, t):
                link(V.tensor_reduce(peak[:, i, n:n + 1], t, X, ALU.max, apply_absolute_value=True))

            dve.wait_ge(cond_T, 1)
            V.tensor_scalar(wcT[:, :], banks[0][:, 0:P], 1.0 / float(P) ** 0.5, None, ALU.mult).then_inc(cond_sb, 1)
            V.tensor_copy(yT[:, :], banks[0][:, P:P + B]).then_inc(cond_sb, 1)
            dve.wait_ge(cond_sb, 2)
            V.tensor_tensor(wc2[:, :], wcT[:, :], wcT[:, :], ALU.mult).then_inc(norm_in, 1)
            V.tensor_tensor(y2[:, :], yT[:, :], yT[:, :], ALU.mult).then_inc(norm_in, 1)
            for b in range(WY_V):
                V.tensor_scalar(wyT[:, b, :], wcT[:, :], yT[:, b:b + 1], None, ALU.mult).then_inc(wy_v, 1)
                if b == 5:
                    dve.wait_ge(norm_mm, 1)
                    V.tensor_scalar(nrm[:, 0, :], banks[1][:, 0:B], 1e-8, None, ALU.add).then_inc(norm_sb, 1)
            dve.wait_ge(norm_sb, 1)
            dve.wait_ge(root_done, 1)
            link(V.reciprocal(nrm[:, 2, :], nrm[:, 1, :]))
            link(V.tensor_tensor(nrm[:, 3, :], nrm[:, 2, :], nrm[:, 2, :], ALU.mult))
            link(V.scalar_tensor_tensor(nrm[:, 4, :], nrm[:, 3, :], -0.5, nrm[:, 0, :], ALU.mult, ALU.mult))
            link(V.tensor_scalar(nrm[:, 3, :], nrm[:, 4, :], 1.5, None, ALU.add))
            link(V.tensor_tensor(nrm[:, 1, :], nrm[:, 3, :], nrm[:, 2, :], ALU.mult))
            dve.wait_ge(ld_w0, 48)
            wb = wn[:, :, :].rearrange("p n (k i) -> p (n k) i", i=WBLK)
            link(V.tensor_reduce(ws[:, 0, :], wb, X, ALU.max, apply_absolute_value=True))
            link(V.tensor_scalar(ws[:, 0, :], ws[:, 0, :], 1.0 / 7.0, TINY, ALU.mult, ALU.max))
            link(V.tensor_scalar(ws[:, 2, :], ws[:, 0, :], WS, None, ALU.mult))
            V.reciprocal(ws[:, 1, :], ws[:, 0, :]).then_inc(w_scales, 1)
            for k in range(NK):
                dve.wait_ge(c_mm, k + 1)
                V.tensor_tensor(c32[:, 4 * k:4 * k + 4, :], batches(banks[k][:, :]),
                                nrm[:, 1, 4 * k:4 * k + 4].unsqueeze(2).to_broadcast([P, 4, P]),
                                ALU.mult).then_inc(c_sb, 1)
                dve.wait_ge(c_sb, k + 1)
                block_peak(0, k, c32[:, 4 * k:4 * k + 4, :].rearrange("p b l -> p (b l)"))
            peak_to_scale(0, NK, lambda u: link(V.memset(u, 1.0)))
            for k in range(NK):
                ck = c32[:, 4 * k:4 * k + 4, :]
                if k in Q_HI_SCALAR:
                    dve.wait_ge(q_hi_s, Q_HI_SCALAR.index(k) + 1)
                else:
                    dve.wait_ge(cq_done, k + 1)
                    V.tensor_scalar(time_major(qhi, k), ck, -MAGIC, None, ALU.add).then_inc(q_hi_v, 1)
                    dve.wait_ge(q_hi_v, k + 1)
                V.scalar_tensor_tensor(time_major(qlo, k), ck, -MAGIC, time_major(qhi, k), ALU.add,
                                       ALU.subtract).then_inc(q_done, 1)
                for n in range(3) if k == 1 else ():
                    dve.wait_ge(wT_hi_done, n + 1)
                    wj = slice(NJ * n, NJ * (n + 1))
                    V.tensor_tensor(wT_lo[:, wj, :].rearrange("p j o -> p (j o)"), banks[4 + n][:, 0:NJ * P],
                                    wT_hi[:, wj, :].rearrange("p j o -> p (j o)"), ALU.subtract).then_inc(wT_done, 1)

            for i, t in ((1, gate2), (2, up2)):
                for k in range(NK):
                    dve.wait_ge(gu_sb, (i - 1) * NJ * NK + NJ * (k + 1))
                    link(V.tensor_reduce(peak[:, i, k:k + 1], tokens(t, k), XY, ALU.max, apply_absolute_value=True))
                    if i == 1 and k == 0:
                        dve.wait_ge(misc_T, 1)
                        V.tensor_copy(miscT[:, :], banks[3][:, 0:NM]).then_inc(misc_sb, 1)
                        dve.wait_ge(misc_sb, 1)
                        link(V.tensor_scalar(rw[:, :], miscT[:, SLOTS + 1:NM], WS, None, ALU.mult))
                        link(V.tensor_scalar(rw_hi[:, :], rw[:, :], 1.0, None, ALU.mult))
                        link(V.tensor_tensor(rw_lo[:, :], rw[:, :], rw_hi[:, :], ALU.subtract))
                peak_to_scale(i, NK, lambda u: link(V.tensor_scalar(u, sc[:, 0, 2:3], 1.0 / WS, None, ALU.mult)))
            for n in range(NJ):
                dve.wait_ge(sig_done, n + 1)
                link(V.tensor_scalar(third(sig2, n), third(sig2, n), SIG_MAX, SIG_MAGIC, ALU.min, ALU.add))
                V.tensor_tensor(third(sig2, n), q16(third(gate2, n)), q16(third(sig2, n), U16), ALU.mult).then_inc(g2_done, 1)
                dve.wait_ge(g2_done, n + 1)
                block_peak(3, n, third(sig2, n))
            peak_to_scale(3, NJ, lambda u: link(V.tensor_scalar(u, sc[:, 1, 2:3], 1.0 / 65536.0, None, ALU.mult)))
            dve.wait_ge(upq, NJ)
            done = 0
            for n in range(2 * NJ):
                if n % 3 != 1:
                    dve.wait_ge(g2q, n + 1)
                    V.tensor_tensor(sixth(up2, n), q16(sixth(sig2, n)), q16(sixth(up2, n)), ALU.mult).then_inc(p_done, 1)
                    done += 1
                    dve.wait_ge(p_done, done)
                    block_peak(4, n, sixth(up2, n))
                if n % 3 == 2:
                    dve.wait_ge(p_pool, n // 3 + 1)
                    block_peak(4, n - 1, sixth(up2, n - 1))
            peak_to_scale(4, 2 * NJ, lambda u: link(V.tensor_tensor(u, sc[:, 3, 2:3], sc[:, 2, 2:3], ALU.mult)))
            link(V.tensor_scalar(pk1[:, 0:1], sc[:, 4, 2:3], 1.0 / WS, None, ALU.mult))

            def quantise_o(k):
                V.tensor_scalar(tokens(up2, k), tokens(up2, k), sc[:, 4, 4:5], MAGIC, ALU.mult, ALU.add).then_inc(oq, 1)
                dve.wait_ge(oq, k + 1)
                V.tensor_scalar(tokens(o_hi, k), tokens(up2.bitcast(I8)[:, 1::4], k), 256.0, None,
                                ALU.mult).then_inc(o_hi_done, 1)

            def make_x1(k):
                dve.wait_ge(down_mm, k + 1)
                V.scalar_tensor_tensor(blk(x1, k), banks[k][:, :], pk1[:, 0:1], blk(xT, k), ALU.mult,
                                       ALU.add).then_inc(x1_done, 1)
                dve.wait_ge(x1_done, k + 1)
                V.tensor_copy(blk(x1_hi, k), blk(x1, k)).then_inc(x1_hi_done, 1)
                dve.wait_ge(x1_hi_done, k + 1)
                V.tensor_tensor(blk(x1_lo, k), blk(x1, k), blk(x1_hi, k), ALU.subtract).then_inc(x1_lo_done, 1)

            for k in range(NK - 1):
                quantise_o(k)
            make_x1(0)
            quantise_o(NK - 1)
            for k in range(1, NK):
                make_x1(k)

            dve.wait_ge(added, NK)
            for n in range(GROUPS_BY[-1], GROUPS):
                dve.wait_ge(nat_T, n + 1)
                V.tensor_copy(wt[:, 1024 * n:1024 * (n + 1)], banks[4 + n % 2][:, :].bitcast(F16)).then_inc(wt_done, 1)

            def take_logits(c):
                dve.wait_ge(logits_mm, c + 1)
                V.tensor_copy(logit[:, :, :].rearrange("p j e -> p (j e)"),
                              ps_logits[:, 0:TILES * E]).then_inc(logit_sb, 1)

            def find_top():
                for j in range(TILES):
                    V.max(top[:, j, :], logit[:, j, :]).then_inc(top_done, 1)

            def find_experts():
                V.tensor_tensor(mixd[:, 0, :], top[:, :, 0], top[:, :, 1], ALU.subtract).then_inc(margin_done, 1)
                for j in range(TILES):
                    V.max_index(topi[:, j, :], top[:, j, :], logit[:, j, :]).then_inc(top_done, 1)

            def mark_experts():
                for a in range(2):
                    V.tensor_tensor(pick[:, a, :, :], topi[:, :, a:a + 1].to_broadcast([P, TILES, E]),
                                    experts[:, :].unsqueeze(1).to_broadcast([P, TILES, E]),
                                    ALU.is_equal).then_inc(pick_done, 1)

            def mix(c):
                dve.wait_ge(mix_done, c + 1)
                V.tensor_scalar(mixd[:, 2, :], mixd[:, 1, :], 0.5 / WS, 0.5 / WS, ALU.mult, ALU.add).then_inc(pick_done, 1)
                V.tensor_scalar(mixd[:, 3, :], mixd[:, 1, :], -0.5 / WS, 0.5 / WS, ALU.mult, ALU.add).then_inc(pick_done, 1)
                dve.wait_ge(pick_done, 6 * c + 4)
                for a in range(2):
                    V.tensor_tensor(pick[:, a, :, :], pick[:, a, :, :],
                                    mixd[:, 2 + a, :].unsqueeze(2).to_broadcast([P, TILES, E]),
                                    ALU.mult).then_inc(pick_done, 1)
                dve.wait_ge(pick_done, 6 * c + 6)
                V.tensor_tensor(gates[:, bass.ds(c * TILES, TILES), :], pick[:, 0, :, :], pick[:, 1, :, :],
                                ALU.add).then_inc(gates_done, 1)
                dve.wait_ge(gates_done, c + 1)

            def add_gated(c, e, j, par):
                g = gates[:, bass.ds(c * TILES + j, 1), bass.ds(e, 1)].rearrange("p a b -> p (a b)")
                a = acc[:, bass.ds(c * TILES + j, 1), :].rearrange("p a b -> p (a b)")
                V.scalar_tensor_tensor(a, ps_y[par][:, P * j:P * (j + 1)], g, a, ALU.mult, ALU.add).then_inc(added, 1)

            def pair(c, e2, prev, rnn):
                first = isinstance(e2, int)
                for s in range(2 * NF):
                    f, par = s % NF, s // NF
                    slot = c * SLOTS + e2 * 2 * NF + s
                    if first and s == 1:
                        take_logits(c)
                    if first and s == 2:
                        dve.wait_ge(logit_sb, c + 1)
                    if first and s == 3:
                        dve.wait_ge(top_done, 2 * TILES * c + TILES)
                    if first and s == 4:
                        dve.wait_ge(top_done, 2 * TILES * (c + 1))
                    if first and s == 6:
                        mix(c)
                    if f % 2 == 0:
                        dve.wait_ge(g32_done, slot + 1)
                        V.tensor_copy(g_hi[:, par, f, :], g32[:, f, :]).then_inc(hi_v, 1)
                        dve.wait_ge(hi_v, c * (SLOTS // 2) + e2 * NF + (s // 2 + 1))
                    else:
                        dve.wait_ge(g_hi_done, c * (SLOTS // 2) + e2 * NF + (s // 2 + 1))
                    V.tensor_tensor(g_lo[:, par, f, :], g32[:, f, :], g_hi[:, par, f, :],
                                    ALU.subtract).then_inc(g_lo_done, 1)
                    if first and s == 2:
                        find_top()
                    if first and s == 3:
                        find_experts()
                    if first and s == 4:
                        mark_experts()
                    if prev and f < 2:
                        cc, e = (c - 1, E - 2 + par) if first else (c, e2 * 2 - 2 + par)
                        if f == 0:
                            dve.wait_ge(y_mm, slot - NF)
                            dve.wait_ge(added, c * E * TILES + e2 * 2 * TILES + (NK - 2 * TILES + par * TILES))
                        for j in ((0,), range(1, TILES))[f]:
                            add_gated(cc, e, j, par)

            chunks(dve, pair)
            for par in range(2):
                dve.wait_ge(y_mm, CH * SLOTS - NF + par * NF)
                dve.wait_ge(added, NK + (CH * E - 2 + par) * TILES)
                for j in range(TILES):
                    add_gated(CH - 1, E - 2 + par, j, par)

        @block.tensor
        def _(pe):
            def mm(o, l, r, start, stop=True):
                return nc.tensor.matmul(o, l, r, start=start, stop=stop, skip_group_check=True)

            def mm3(o, l_hi, l_lo, r_hi, r_lo, start=True):
                mm(o, l_hi, r_hi, start)
                mm(o, l_lo, r_hi, False)
                return mm(o, l_hi, r_lo, False)

            def spread_peak(i):
                pe.wait_ge(pk_part, i + 1)
                mm(ps_pk[:, 0:P], pk1[:, i:i + 1].to_broadcast([P, P]), ident[:, :], True).then_inc(pk_all, 1)

            def transpose_group(n):
                if n % (GROUPS // 2) == 0:
                    pe.wait_ge(nat_done, 8 if n == 0 else 16)
                if n >= 2:
                    pe.wait_ge(wt_done, n - 1)
                if n == GROUPS_BY[-1]:
                    pe.wait_ge(added, 2)
                for m in range(8):
                    last = nc.tensor.transpose(banks[4 + n % 2][:, :].bitcast(F16)[:, P * m:P * (m + 1)],
                                               nat[:, 1024 * n + P * m:1024 * n + P * (m + 1)], ident16[:, :])
                last.then_inc(nat_T, 1)

            pe.wait_ge(consts, 4)
            pe.wait_ge(ld_cond, 32)
            nc.tensor.transpose(banks[0][:, 0:P], wc[:, :], ident[:, :])
            nc.tensor.transpose(banks[0][:, P:P + B], y_sb[:, :], ident[0:B, 0:B]).then_inc(cond_T, 1)
            pe.wait_ge(norm_in, 2)
            mm(banks[1][:, 0:B], wc2[:, :], y2[:, :], True).then_inc(norm_mm, 1)
            for b in range(B):
                if b % 4 == 0:
                    pe.wait_ge(ld_x[b // 4], 16)
                if b == 4:
                    pe.wait_ge(norm_sb, 1)
                pe.wait_ge(*((wy_v, b + 1) if b < WY_V else (wy_s, b - WY_V + 1)))
                last = mm(banks[b // 4][:, P * (b % 4):P * (b % 4 + 1)], wyT[:, b, :], x_sb[:, b, :], True)
                if b % 4 == 3:
                    last.then_inc(c_mm, 1)
            for b in range(B):
                last = nc.tensor.transpose(banks[4 + b // 4][:, P * (b % 4):P * (b % 4 + 1)], x_sb[:, b, :], ident[:, :])
                if b % 4 == 3:
                    last.then_inc(xT_mm, 1)
            for k in range(NK):
                pe.wait_ge(c_sb, k + 1)
                for b in range(4 * k, 4 * k + 4):
                    last = nc.tensor.transpose(banks[k][:, P * (b % 4):P * (b % 4 + 1)], c32[:, b, :], ident[:, :])
                last.then_inc(cT_mm, 1)
            pe.wait_ge(xT_sb, NK)
            spread_peak(0)
            pe.wait_ge(wdeq, 1)
            for n in range(3):
                for j in range(NJ):
                    last = nc.tensor.transpose(banks[4 + n][:, P * j:P * (j + 1)], wn[:, NJ * n + j, :], ident[:, :])
                last.then_inc(wT_mm, 1)
            for n in range(2 * NJ * NK):
                t, k, j = n // (NJ * NK), n % (NJ * NK) // NJ, n % NJ
                if n < NJ:
                    pe.wait_ge(wT_done, n + 1)
                if n == 0:
                    pe.wait_ge(q_done, NK)
                if n >= 6:
                    pe.wait_ge(gu_sb, n - 5)
                if n == 2 * NJ:
                    pe.wait_ge(ld_misc, 48)
                    pe.wait_ge(cq_done, NK)
                    nc.tensor.transpose(banks[3][:, 0:NM], misc[:, :], ident[0:NM, 0:NM]).then_inc(misc_T, 1)
                if n == NJ * NK + 5:
                    spread_peak(1)
                w = NJ * t + j
                mm3(banks[GU_BANKS[n % 6]][:, :], wT_hi[:, w, :], wT_lo[:, w, :], blk(qhi, k), blk(qlo, k)).then_inc(gu_mm, 1)
            pe.wait_ge(gu_sb, 2 * NJ * NK)
            spread_peak(2)
            for n in range(GROUPS_BY[0]):
                transpose_group(n)
            spread_peak(3)
            for n in range(GROUPS_BY[0], GROUPS_BY[-1]):
                transpose_group(n)
            spread_peak(4)

            def input_part(c):
                at = bass.ds(c * CT, CT)
                mm3(ps_rnn[:, 0:CT], wx_hi[:, :], wx_lo[:, :], x1_hi[:, at], x1_lo[:, at])

            w_h32 = wxh[:, 1, :]

            def first_step(r):
                if r:
                    pe.wait_ge(h32_done, r)
                state = h32[:, B * (r - 1):B * r] if r else yT[:, :]
                mm(ps_rnn[:, B * r:B * (r + 1)], w_h32, state, False).then_inc(rnn_mm, 1)

            for k in range(NK):
                if k == 2:
                    pe.wait_ge(small_w, 2)
                    pe.wait_ge(b2_moved, 16)
                    pe.wait_ge(x1_lo_done, 1)
                    input_part(0)
                pe.wait_ge(o_hi_done, k + 1)
                for p, (part, w) in enumerate(((o_hi, wT_hi), (o_hi, wT_lo), (o_lo, wT_hi), (o_lo, wT_lo))):
                    if p == 2:
                        pe.wait_ge(o_lo_done, k + 1)
                    for j in range(NJ):
                        if k >= 2 and (p * NJ + j) % 4 == 0:
                            first_step((k - 2) * NJ + (p * NJ + j) // 4)
                        last = mm(banks[k][:, :], w[:, 2 * NJ + j, :], blk(part, j * NK + k), p == 0 and j == 0)
                last.then_inc(down_mm, 1)
            first_step(EARLY_STEPS - 2)
            pe.wait_ge(x1_done, NK)
            for j in range(CH * TILES):
                if j == CH * TILES // 2:
                    first_step(EARLY_STEPS - 1)
                last = nc.tensor.transpose(banks[4 + j // 4][:, P * (j % 4):P * (j % 4 + 1)], x1[:, P * j:P * (j + 1)], ident[:, :])
                if j % 4 == 3:
                    last.then_inc(x1T_mm, 1)

            for r in range(EARLY_STEPS, STEPS):
                first_step(r)
                if (r - EARLY_STEPS) % 3 == 0 and GROUPS_BY[-1] + (r - EARLY_STEPS) // 3 < GROUPS:
                    transpose_group(GROUPS_BY[-1] + (r - EARLY_STEPS) // 3)

            def logits(c):
                for j in range(TILES):
                    t = bass.ds(c * CT + P * j, P)
                    o = ps_logits[:, E * j:E * (j + 1)]
                    mm(o, h_hi[:, t], rw_hi[:, :], j == 0)
                    mm(o, h_hi[:, t], rw_lo[:, :], False)
                    mm(o, h_lo[:, t], rw_hi[:, :], False)
                    last = mm(o, h_lo[:, t], rw_lo[:, :], False)
                last.then_inc(logits_mm, 1)

            def start_y(e, par):
                rows = b2s[:, bass.ds(e, 1), :].to_broadcast([2, TILES, P])
                mm(ps_y[par][:, 0:CT].rearrange("p (j h) -> p j h", h=P), ones2[:, :], rows, True)

            def down(e, par, f):
                w = bass.ds(e * FF + f * P, P)
                for j in range(TILES):
                    o = ps_y[par][:, P * j:P * (j + 1)]
                    tile = slice(P * j, P * (j + 1))
                    mm(o, g_hi[:, par, f, tile], w2T_hi[:, w], False)
                    mm(o, g_hi[:, par, f, tile], w2T_lo[:, w], False)
                    last = mm(o, g_lo[:, par, f, tile], w2T_hi[:, w], False)
                last.then_inc(y_mm, 1)

            def pair(c, e2, prev, rnn):
                first = isinstance(e2, int)
                for s in range(2 * NF):
                    f, par = s % NF, s // NF
                    slot = c * SLOTS + e2 * 2 * NF + s
                    if rnn and first and s == 0:
                        pe.wait_ge(h32_done, c * STEPS + STEPS)
                        input_part(c + 1)
                    if prev or s >= NF:
                        e = e2 * 2 + par - 1 if not first else (E - 1 if par == 0 else 0)
                        if f == 0:
                            if prev:
                                pe.wait_ge(added, c * E * TILES + e2 * 2 * TILES + (NK - 2 * TILES + par * TILES))
                            start_y(e, 1 - par)
                        pe.wait_ge(g_lo_done, slot - NF + 1)
                        down(e, 1 - par, f)
                    if rnn:
                        pe.wait_ge(h32_done, slot + STEPS)
                        mm(ps_rnn[:, bass.ds(e2 * 2 * NF * B + s * B, B)], w_h32, h32[:, bass.ds((slot + STEPS) * B - B, B)],
                           False).then_inc(rnn_mm, 1)
                    if first and s == 0:
                        pe.wait_ge(h_lo_done, c * (STEPS // 4) + STEPS // 4)
                    w = bass.ds(e2 * 2 * FF + s * P, P)
                    t = bass.ds(c * CT, CT)
                    mm3(ps_h[f][:, 0:CT], w1T_hi[:, w], w1T_lo[:, w], h_hi[:, t], h_lo[:, t]).then_inc(hid_mm, 1)
                    if first and s == 0:
                        if prev:
                            pe.wait_ge(logit_sb, c)
                        logits(c)

            pe.wait_ge(added, NK)
            pe.wait_ge(wt_done, GROUPS)
            chunks(pe, pair)
            pe.wait_ge(added, NK + (CH * E - 3 + 1) * TILES)
            start_y(E - 1, 1)
            for f in range(NF):
                pe.wait_ge(g_lo_done, CH * SLOTS - NF + f + 1)
                down(E - 1, 1, f)


def kernel(x, cond_1024, L0_cond_weight, L0_ffn_w_gate, L0_ffn_w_up, L0_ffn_w_down, L1_cond_Wx, L1_cond_Wh, L1_cond_b,
           L1_ffn_router_w, L1_ffn_w1, L1_ffn_b1, L1_ffn_w2, L1_ffn_b2):
    import numpy as np
    import concourse.bacc as bacc
    from concourse.bass_utils import run_bass_kernel_spmd

    nc = bacc.Bacc("TRN2", target_bir_lowering=False, num_devices=1)
    given = {"x": x, "cond": cond_1024, "w_cond": L0_cond_weight, "w_gate": L0_ffn_w_gate, "w_up": L0_ffn_w_up,
             "w_down": L0_ffn_w_down, "w_x": L1_cond_Wx, "w_h": L1_cond_Wh, "b_h": L1_cond_b,
             "w_router": L1_ffn_router_w, "w1": L1_ffn_w1, "b1": L1_ffn_b1, "w2": L1_ffn_w2, "b2": L1_ffn_b2}
    arrays = {f"in_{n}": np.ascontiguousarray(a) for n, a in given.items()}
    aps = [nc.dram_tensor(n, a.shape, mybir.dt.from_np(a.dtype), kind="ExternalInput").ap() for n, a in arrays.items()]
    out = nc.dram_tensor("out_block", x.shape, F32, kind="ExternalOutput").ap()
    program(nc, *aps, out)
    r = run_bass_kernel_spmd(nc, [arrays], core_ids=[0])
    return r.results[0]["out_block"]
```

```python
from contextlib import ExitStack

import concourse.bass as bass
from concourse import mybir

F32, F16 = mybir.dt.float32, mybir.dt.float16
I8, U8 = mybir.dt.int8, mybir.dt.uint8
I16, U16 = mybir.dt.int16, mybir.dt.uint16
ALU = mybir.AluOpType
ACT = mybir.ActivationFunctionType
X, XY = mybir.AxisListType.X, mybir.AxisListType.XY

P = 128
B = 16
T = 128
TOK = B * T
INNER = 384
NJ = INNER // P
BANK = 512
NK = TOK // BANK
WBLK = 32
NW = 3 * NJ
E, FF = 8, 512
NF = FF // P
WIDTHS = (256, 384, 512, 512, 384)
CH = len(WIDTHS)
START = [sum(WIDTHS[:c]) for c in range(CH + 1)]
TILES = [w // P for w in WIDTHS]
CT = max(WIDTHS)
CTILES = CT // P
FIRST_STEPS = WIDTHS[0] // B
RNN_SLOTS = ((0, 1, 3, 4, 5, 7), range(8), range(8), (0, 1, 2, 4, 5, 6), ())
RNN_FROM = [FIRST_STEPS + E // 2 * sum(len(n) for n in RNN_SLOTS[:c]) for c in range(CH)]
HI_SCALAR = ((3,), (), (3,), (3,), (0, 1, 3))
TS = P // B
SLOTS = E * NF
WS = 256.0
QMAX = 32767.0
TINY = 1e-12
MAGIC = 12582912.0
SIG_MAGIC = 192.0
SIG_MAX = 65535.0 / 65536.0
C_V = 2
EARLY_STEPS = FIRST_STEPS - NK
PIECE = E * NF * P // 4
GROUPS = 4 * E * NF // 8
GROUPS_BY = (4, 4, 4, 5, 6, 7, 13)
WY_V = 10


def program(nc, x, cond, w_cond, w_gate, w_up, w_down, w_x, w_h, b_h, w_router, w1, b1, w2, b2, out):
    ctx = ExitStack()
    with ctx:
        def sb(name, shape, dt=F32):
            return ctx.enter_context(nc.sbuf_tensor(name, shape, dt))

        def sem(name):
            return ctx.enter_context(nc.semaphore(name))

        def sems(names):
            return [sem(n) for n in names.split()]

        banks = [ctx.enter_context(nc.psum_tensor(f"bank{i}", [P, BANK], F32)) for i in range(8)]

        ident = sb("ident", [P, P])
        ident16 = sb("ident16", [P, P], F16)
        experts = sb("experts", [P, E])
        x_sb = sb("x_sb", [P, B, P])
        xT = sb("xT", [P, TOK])
        wc = sb("wc", [P, P])
        y_sb = sb("y_sb", [B, P])
        wcT = sb("wcT", [P, P])
        yT = sb("yT", [P, B])
        wc2 = sb("wc2", [P, P])
        y2 = sb("y2", [P, B])
        nrm = sb("nrm", [P, 5, B])
        wyT = sb("wyT", [P, B, P])
        c32 = sb("c32", [P, B, P])
        q = sb("q", [P, 2, TOK], F16)
        qhi, qlo = q[:, 0, :], q[:, 1, :]
        wn = sb("wn", [P, NW, P])
        ws = sb("ws", [P, 3, NW * P // WBLK])
        wT_hi = sb("wT_hi", [P, NW, P], F16)
        wT_lo = sb("wT_lo", [P, NW, P], F16)
        big = sb("big", [P, 3 * NJ * TOK])
        gate2, up2, sig2 = (big[:, i * NJ * TOK:(i + 1) * NJ * TOK] for i in range(3))
        peak = sb("peak", [P, 5, NJ * NK])
        pk1 = sb("pk1", [P, 5])
        pkm = sb("pkm", [P, 5])
        sc = sb("sc", [P, 5, 5])
        x1 = c32[:, :, :].rearrange("p b l -> p (b l)")
        x1_hi, x1_lo = (x_sb[:, :, :].rearrange("p b l -> p (b l)").bitcast(F16)[:, i * TOK:(i + 1) * TOK] for i in range(2))
        acc = wyT
        h32 = q[:, :, :].rearrange("p a n -> p (a n)").bitcast(F32)
        wxh = sb("wxh", [P, 2, P])
        wx_hi = sb("wx_hi", [P, P], F16)
        wx_lo = sb("wx_lo", [P, P], F16)
        NM = E * NF + 1 + E
        misc = sb("misc", [NM, P])
        miscT = sb("miscT", [P, NM])
        rw = sb("rw", [P, E])
        rw_hi = sb("rw_hi", [P, E], F16)
        rw_lo = sb("rw_lo", [P, E], F16)
        b2_all = sb("b2_all", [P, E, P])
        stage = sb("stage", [P, 2, PIECE])
        nat = sb("nat", [P, 4 * SLOTS * P], F16)
        wt = sb("wt", [P, 4 * SLOTS * P], F16)
        g32 = sig2[:, 0:NF * CT].rearrange("p (f n) -> p f n", f=NF)
        g_hi, g_lo = (sig2.bitcast(F16)[:, 2 * NF * CT * (i + 1):2 * NF * CT * (i + 2)].rearrange("p (a f n) -> p a f n", a=2, f=NF)
                      for i in range(2))
        h_hi, h_lo = (up2.bitcast(F16)[:, TOK * i:TOK * (i + 1)] for i in range(2))
        b2_prod = gate2[:, 0:E * P].rearrange("p (e n) -> p e n", e=E)
        b2_sum = gate2[:, E * P:E * P + 2 * CT].rearrange("p (a j n) -> p a j n", a=2, n=P)
        logit = sb("logit", [P, CTILES, E])
        top = sb("top", [P, CTILES, 8])
        topi = sb("topi", [P, CTILES, 8], U16)
        mixd = sb("mixd", [P, 4, CTILES])
        pick = sb("pick", [P, 2, CTILES, E])
        gates = sb("gates", [P, TOK // P, E])

        ld_x = [sem(f"ld_x{i}") for i in range(4)]
        ld_cond, ld_w0, ld_misc, ld_wx, ld_b2, ld_stage0, ld_stage1 = sems(
            "ld_cond ld_w0 ld_misc ld_wx ld_b2 ld_stage0 ld_stage1")
        ld_stage = [ld_stage0, ld_stage1]
        consts, cond_T, cond_sb, norm_in, norm_mm, norm_sb, root_done, norm_done = sems(
            "consts cond_T cond_sb norm_in norm_mm norm_sb root_done norm_done")
        xT_mm, xT_sb, wy_v, wy_s, c_mm, c_v, c_s, cT_mm, cq_done, q_hi_v, q_hi_s, q_done = sems(
            "xT_mm xT_sb wy_v wy_s c_mm c_v c_s cT_mm cq_done q_hi_v q_hi_s q_done")
        w_scales, wdeq, wT_mm, wT_hi_done, wT_done, misc_T, misc_sb = sems(
            "w_scales wdeq wT_mm wT_hi_done wT_done misc_T misc_sb")
        pk_part, pk_all, scale_done, dve_step, pool_step = sems("pk_part pk_all scale_done dve_step pool_step")
        gu_mm, gu_sb, gateq, upq, sig_done, g2_done, p_pool, g2q, p_done, oq, o_hi_done, o_lo_done, o_lo_v = sems(
            "gu_mm gu_sb gateq upq sig_done g2_done p_pool g2q p_done oq o_hi_done o_lo_done o_lo_v")
        down_mm, x1_done, x1_hi_done, x1_lo_done, x1T_mm = sems("down_mm x1_done x1_hi_done x1_lo_done x1T_mm")
        nat_done, small_w, nat_T, wt_done = sems("nat_done small_w nat_T wt_done")
        rnn_mm, h32_done, h_hi_done, h_lo_done = sems("rnn_mm h32_done h_hi_done h_lo_done")
        logits_mm, logit_sb, top_done, margin_done, mix_done, pick_done, gates_done = sems(
            "logits_mm logit_sb top_done margin_done mix_done pick_done gates_done")
        hid_mm, g32_done, g_hi_done, hi_v, g_lo_done, y_mm, added, b2_summed, b2_added, stored = sems(
            "hid_mm g32_done g_hi_done hi_v g_lo_done y_mm added b2_summed b2_added stored")

        ps_rnn = banks[0]
        ps_y = [banks[1], banks[2]]
        ps_logits = banks[3]
        ps_h = banks[4:8]
        ps_pk = banks[7]
        Q_HI_SCALAR = (2, 3)
        P_POOL, PEAK_AFTER = (1, 3, 5), (2, 4, 5)
        DOWN_BANKS = [0, 4, 1, 2, 3]
        GU_BANKS = [4, 5, 6, 0, 1, 2]
        w1T_hi, w1T_lo, w2T_hi, w2T_lo = (wt[:, i * SLOTS * P:(i + 1) * SLOTS * P] for i in range(4))

        def q16(t, dt=I16):
            return t.bitcast(dt)[:, 0::2]

        def blk(t, n):
            return t[:, BANK * n:BANK * (n + 1)]

        def third(t, n):
            return t[:, TOK * n:TOK * (n + 1)]

        def group_bank(n):
            return banks[(4 if n < GROUPS_BY[-1] else 1) + n % 2][:, :].bitcast(F16)

        def sixth(t, n):
            return t[:, TOK // 2 * n:TOK // 2 * (n + 1)]

        SIG_FROM = (0, 1, 2, 4, 6)
        SIG_PIECES = len(SIG_FROM) - 1

        def piece(t, n):
            return t[:, TOK // 2 * SIG_FROM[n]:TOK // 2 * SIG_FROM[n + 1]]

        def tokens(t, k):
            return t.rearrange("p (j n) -> p j n", j=NJ)[:, :, BANK * k:BANK * (k + 1)]

        def chunk_of(t, c):
            return t.rearrange("p (j n) -> p j n", j=NJ)[:, :, START[c]:START[c + 1]]

        def time_major(t, k):
            return t.rearrange("p (t b) -> p b t", b=B)[:, 4 * k:4 * k + 4, :]

        def batches(t):
            return t.rearrange("p (b n) -> p b n", n=P)

        o_hi = gate2.bitcast(F16)[:, 0:NJ * TOK]
        o_lo = gate2.bitcast(F16)[:, NJ * TOK:2 * NJ * TOK]

        def chunks(eng, pair):
            for c in range(CH):
                pair(c, 0, c > 0)
                with eng.Fori(1, E // 2 - (c == CH - 1)) as e2:
                    pair(c, e2, True)
            pair(CH - 1, E // 2 - 1, True)

        def is_first(e2):
            return isinstance(e2, int) and e2 == 0

        def added_before(c, e2, par):
            if is_first(e2):
                return NK + E * START[c] // P - (2 - par) * TILES[c - 1]
            return e2 * (2 * TILES[c]) + (NK + E * START[c] // P - (2 - par) * TILES[c])

        def rnn_step(c, e2, s):
            if s not in RNN_SLOTS[c]:
                return None
            return e2 * len(RNN_SLOTS[c]) + (RNN_FROM[c] + RNN_SLOTS[c].index(s))

        def rnn_column(c, step):
            return (step + -RNN_FROM[c]) * B

        def hi_made(c, e2, s, scalar):
            made = [sum((f in HI_SCALAR[i]) == scalar for f in range(NF)) for i in range(CH)]
            return e2 * (2 * made[c]) + (E * sum(made[:c]) + s // NF * made[c]
                                         + sum((f in HI_SCALAR[c]) == scalar for f in range(s % NF + 1)))

        block = ctx.enter_context(nc.Block())

        @block.sync
        def _(sp):
            sp.dma_start(wc[:, :], w_cond.rearrange("a o i c -> (a o) (i c)")).then_inc(ld_cond, 16)
            sp.dma_start(y_sb[:, :], cond).then_inc(ld_cond, 16)
            for h in range(4):
                sp.dma_start(x_sb[:, 4 * h:4 * h + 4, :],
                             x[4 * h:4 * h + 4].rearrange("b p l -> p b l")).then_inc(ld_x[h], 16)
            sp.dma_start(wn[:, 0:NJ, :], w_gate.rearrange("(j p) i -> p j i", p=P)).then_inc(ld_w0, 16)
            sp.dma_start(wn[:, NJ:2 * NJ, :], w_up.rearrange("(j p) i -> p j i", p=P)).then_inc(ld_w0, 16)
            sp.dma_start(wn[:, 2 * NJ:NW, :], w_down.rearrange("p (j i) -> p j i", j=NJ)).then_inc(ld_w0, 16)
            sp.dma_start(wxh[:, 0, :], w_x).then_inc(ld_wx, 16)
            sp.dma_start(wxh[:, 1, :], w_h).then_inc(ld_wx, 16)
            sp.dma_start(misc[0:E * NF, :], b1.rearrange("e (f p) -> (e f) p", p=P)).then_inc(ld_misc, 16)
            sp.dma_start(misc[E * NF:E * NF + 1, :], b_h.rearrange("(a n) -> a n", a=1)).then_inc(ld_misc, 16)
            sp.dma_start(misc[E * NF + 1:NM, :], w_router).then_inc(ld_misc, 16)
            sp.dma_start(b2_all[:, :, :].rearrange("p e n -> p (e n)"),
                         b2.rearrange("e n -> (e n)").partition_broadcast(P)).then_inc(ld_b2, 16)
            for i in range(8):
                if i >= 2:
                    sp.wait_ge(nat_done, 2 * (i - 1))
                if i < 4:
                    src = w1[2 * i:2 * i + 2].rearrange("e (f p) h -> p (e f) h", p=P)
                    dst = stage[:, i % 2, :].rearrange("p (n h) -> p n h", h=P)
                else:
                    src = w2[2 * (i - 4):2 * (i - 4) + 2].rearrange("e h f -> h e f")
                    dst = stage[:, i % 2, :].rearrange("p (e f) -> p e f", f=FF)
                sp.dma_start(dst, src).then_inc(ld_stage[i % 2], 16)
            for c in range(CH):
                for j in range(TILES[c]):
                    tile = START[c] // P + j
                    if c < CH - 1:
                        sp.wait_ge(b2_added, c + 1)
                    else:
                        sp.wait_ge(added, NK + E * TOK // P - TILES[c] + j + 1)
                    sp.dma_start(out[:, TS * tile:TS * (tile + 1), :].rearrange("b t h -> t b h"),
                                 acc[:, tile, :]).then_inc(stored, 16)
            sp.wait_ge(stored, 16 * TOK // P)

        @block.gpsimd
        def _(pool):
            pool_n = [0]

            def link(ins):
                pool_n[0] += 1
                ins.then_inc(pool_step, 1)
                pool.wait_ge(pool_step, pool_n[0])

            G = nc.gpsimd
            link(G.memset(ident[:, :], 0.0))
            G.affine_select(out=ident[:, :], in_=ident[:, :], compare_op=ALU.not_equal, fill=1.0, base=0,
                            pattern=[[-1, P]], channel_multiplier=1).then_inc(consts, 1)
            G.iota(experts[:, :], [[1, E]], base=0, channel_multiplier=0,
                   allow_small_or_imprecise_dtypes=True).then_inc(consts, 1)
            pool.wait_ge(consts, 2)
            G.tensor_copy(ident16[:, :], ident[:, :]).then_inc(consts, 1)

            def split(hi, lo, src):
                link(G.tensor_scalar(src, src, WS, 0.0, ALU.mult, ALU.add))
                link(G.tensor_scalar(hi, src, 1.0, 0.0, ALU.mult, ALU.add))
                return G.tensor_tensor(lo, src, hi, ALU.subtract)

            pool.wait_ge(ld_wx, 32)
            split(wx_hi[:, :], wx_lo[:, :], wxh[:, 0, :]).then_inc(small_w, 1)
            G.tensor_scalar(wxh[:, 1, :], wxh[:, 1, :], WS, 0.0, ALU.mult, ALU.add).then_inc(small_w, 1)
            pool.wait_ge(w_scales, 1)
            for n, to in ((0, NJ), (NJ, NW)):
                wb = wn[:, n:to, :].rearrange("p n (k i) -> p (n k) i", i=WBLK)
                inverse, scale = (ws[:, i, 4 * n:4 * to].unsqueeze(2).to_broadcast([P, 4 * (to - n), WBLK]) for i in (1, 2))
                link(G.tensor_tensor(wb, wb, inverse, ALU.mult))
                link(G.tensor_scalar(wb, wb, 1.0, MAGIC, ALU.mult, ALU.add))
                link(G.tensor_scalar(wb, wb, 1.0, -MAGIC, ALU.mult, ALU.add))
                G.tensor_tensor(wb, wb, scale, ALU.mult).then_inc(wdeq, 1)
            pool.wait_ge(ld_b2, 16)
            link(G.tensor_scalar(b2_all[:, :, :], b2_all[:, :, :], WS, 0.0, ALU.mult, ALU.add))
            for i in range(8):
                pool.wait_ge(ld_stage[i % 2], 16 * (i // 2 + 1))
                for n in range(PIECE // BANK):
                    at = 2 * (i // 4) * SLOTS * P + PIECE * (i % 4) + BANK * n
                    split(nat[:, at:at + BANK], nat[:, at + SLOTS * P:at + SLOTS * P + BANK],
                          stage[:, i % 2, BANK * n:BANK * (n + 1)]).then_inc(nat_done, 1)
            pool.wait_ge(upq, NJ)
            for n in P_POOL:
                link(G.tensor_scalar(sixth(up2, n), sixth(up2, n), 1.0, -MAGIC, ALU.mult, ALU.add))
            for n in P_POOL:
                pool.wait_ge(g2q, n)
                link(G.tensor_scalar(sixth(sig2, n), sixth(sig2, n), 1.0, -MAGIC, ALU.mult, ALU.add))
                G.tensor_tensor(sixth(up2, n), sixth(sig2, n), sixth(up2, n), ALU.mult).then_inc(p_pool, 1)
            pool.wait_ge(o_hi_done, CH)
            pool.wait_ge(o_lo_done, CH - 1)
            pool.wait_ge(o_lo_v, 1)
            def split_states(i):
                pool.wait_ge(h32_done, 4 * i + 4)
                at = slice(4 * i * B, 4 * (i + 1) * B)
                G.tensor_copy(h_hi[:, at], h32[:, at]).then_inc(h_hi_done, 1)
                pool.wait_ge(h_hi_done, i + 1)
                G.tensor_tensor(h_lo[:, at], h32[:, at], h_hi[:, at], ALU.subtract).then_inc(h_lo_done, 1)

            def sum_b2(c, j):
                tile = START[c] // P + j
                gate = gates[:, tile, :].unsqueeze(2).to_broadcast([P, E, P])
                link(G.tensor_tensor(b2_prod, b2_all[:, :, :], gate, ALU.mult))
                for n in (4, 2):
                    link(G.tensor_tensor(b2_prod[:, 0:n, :], b2_prod[:, 0:n, :], b2_prod[:, n:2 * n, :], ALU.add))
                G.tensor_tensor(b2_sum[:, c % 2, j, :], b2_prod[:, 0, :], b2_prod[:, 1, :], ALU.add).then_inc(b2_summed, 1)
                pool.wait_ge(b2_summed, tile + 1)

            done = FIRST_STEPS // 4
            for i in range(done):
                split_states(i)
            for c in range(CH):
                to = (RNN_FROM[c + 1] if c < CH - 1 else T) // 4
                for i in range(done, min(done + 3, to)):
                    split_states(i)
                done = min(done + 3, to)
                pool.wait_ge(gates_done, c + 1)
                if c >= 2:
                    pool.wait_ge(b2_added, c - 1)
                for j in range(TILES[c]):
                    sum_b2(c, j)
                    if done < to:
                        split_states(done)
                        done += 1
                for i in range(done, to):
                    split_states(i)
                done = to

        @block.scalar
        def _(act):
            A = nc.scalar.activation

            def take_group(n):
                act.wait_ge(nat_T, n + 1)
                A(wt[:, 1024 * n:1024 * (n + 1)], group_bank(n), ACT.Copy).then_inc(wt_done, 1)

            nc.scalar.preload_act_table(ACT.Sqrt)
            act.wait_ge(cond_sb, 2)
            for b in range(WY_V, B):
                A(wyT[:, b, :], wcT[:, :], ACT.Copy, scale=yT[:, b:b + 1]).then_inc(wy_s, 1)
            act.wait_ge(norm_sb, 1)
            A(nrm[:, 1, :], nrm[:, 0, :], ACT.Sqrt).then_inc(root_done, 1)
            nc.scalar.preload_act_table(ACT.Sigmoid)
            act.wait_ge(norm_done, 1)
            for k in range(C_V, NK):
                act.wait_ge(c_mm, k + 1)
                for b in range(4 * k, 4 * k + 4):
                    last = A(c32[:, b, :], banks[k][:, P * (b % 4):P * (b % 4 + 1)], ACT.Copy, scale=nrm[:, 1, b:b + 1])
                last.then_inc(c_s, 1)
            for k in range(NK):
                act.wait_ge(xT_mm, k + 1)
                A(time_major(xT[:, :], k), batches(banks[4 + k][:, :]), ACT.Copy).then_inc(xT_sb, 1)
            act.wait_ge(scale_done, 1)
            def take_weights(n):
                act.wait_ge(wT_mm, n + 1)
                A(wT_hi[:, NJ * n:NJ * (n + 1), :].rearrange("p j o -> p (j o)"), banks[4 + n][:, 0:NJ * P],
                  ACT.Copy).then_inc(wT_hi_done, 1)

            for k in range(NK):
                act.wait_ge(cT_mm, k + 1)
                A(c32[:, 4 * k:4 * k + 4, :].rearrange("p b l -> p (b l)"), banks[k][:, :], ACT.Copy,
                  scale=sc[:, 0, 4:5], bias=MAGIC).then_inc(cq_done, 1)
                if k == 1:
                    take_weights(0)
            take_weights(1)
            take_weights(2)
            for i, k in enumerate(Q_HI_SCALAR):
                act.wait_ge(cq_done, NK)
                A(time_major(qhi, k), c32[:, 4 * k:4 * k + 4, :], ACT.Copy, bias=-MAGIC).then_inc(q_hi_s, 1)
            for n in range(2 * NJ * NK):
                act.wait_ge(gu_mm, n + 1)
                t, k, j = (gate2, up2)[n // (NJ * NK)], n % (NJ * NK) // NJ, n % NJ
                A(blk(t, j * NK + k), banks[GU_BANKS[n % 6]][:, :], ACT.Copy).then_inc(gu_sb, 1)
            act.wait_ge(scale_done, 2)
            for n in range(SIG_PIECES):
                A(piece(gate2, n), piece(gate2, n), ACT.Copy, scale=sc[:, 1, 4:5], bias=MAGIC).then_inc(gateq, 1)
                act.wait_ge(gateq, n + 1)
                A(piece(sig2, n), q16(piece(gate2, n)), ACT.Sigmoid, scale=sc[:, 1, 2:3]).then_inc(sig_done, 1)
            act.wait_ge(scale_done, 3)
            for n in range(NJ):
                A(third(up2, n), third(up2, n), ACT.Copy, scale=sc[:, 2, 4:5], bias=MAGIC).then_inc(upq, 1)
            nc.scalar.preload_act_table(ACT.Gelu)
            for n in range(GROUPS_BY[0]):
                take_group(n)
            act.wait_ge(scale_done, 4)
            for n in range(2 * NJ):
                if n > 0:
                    A(sixth(sig2, n), sixth(sig2, n), ACT.Copy, scale=sc[:, 3, 4:5], bias=MAGIC).then_inc(g2q, 1)
                for m in range(GROUPS_BY[n], GROUPS_BY[n + 1]):
                    take_group(m)
            def low_byte(c):
                act.wait_ge(oq, c + 1)
                A(chunk_of(o_lo, c), chunk_of(up2.bitcast(U8)[:, 0::4], c), ACT.Copy).then_inc(o_lo_done, 1)

            for c in range(CH - 1):
                low_byte(c)
            act.wait_ge(misc_sb, 1)
            bias_h = miscT[:, SLOTS:SLOTS + 1]

            def first_step(r):
                act.wait_ge(rnn_mm, r + 1)
                at = slice(r * B, (r + 1) * B)
                A(h32[:, at], ps_rnn[:, at], ACT.Tanh, bias=bias_h, scale=1 / WS).then_inc(h32_done, 1)

            for r in range(EARLY_STEPS):
                first_step(r)
            for k in range(NK):
                first_step(EARLY_STEPS + k)
                act.wait_ge(x1T_mm, k + 1)
                A(acc[:, 4 * k:4 * k + 4, :].rearrange("p j h -> p (j h)"), banks[4 + k][:, :], ACT.Copy).then_inc(added, 1)

            def pair(c, e2, prev):
                first = is_first(e2)
                w = WIDTHS[c]
                for s in range(2 * NF):
                    f = s % NF
                    slot = c * SLOTS + e2 * 2 * NF + s
                    step = rnn_step(c, e2, s)
                    if step is not None:
                        act.wait_ge(rnn_mm, step + 1)
                        A(h32[:, bass.ds(step * B, B)], ps_rnn[:, bass.ds(rnn_column(c, step), B)], ACT.Tanh,
                          bias=bias_h, scale=1 / WS).then_inc(h32_done, 1)
                    act.wait_ge(hid_mm, slot + 1)
                    bias = miscT[:, bass.ds(e2 * 2 * NF + s, 1)]
                    A(g32[:, f, 0:w], ps_h[f][:, 0:w], ACT.Gelu, bias=bias, scale=1 / WS).then_inc(g32_done, 1)
                    if f in HI_SCALAR[c]:
                        A(g_hi[:, s // NF, f, 0:w], ps_h[f][:, 0:w], ACT.Gelu, bias=bias, scale=1 / WS).then_inc(g_hi_done, 1)
                    if first and s == NF + 1:
                        act.wait_ge(margin_done, c + 1)
                        A(mixd[:, 1, 0:TILES[c]], mixd[:, 0, 0:TILES[c]], ACT.Tanh, scale=0.5 / WS).then_inc(mix_done, 1)

            chunks(act, pair)

        @block.vector
        def _(dve):
            dve_n = [0]

            def link(ins):
                dve_n[0] += 1
                ins.then_inc(dve_step, 1)
                dve.wait_ge(dve_step, dve_n[0])

            V = nc.vector

            def peak_to_scale(i, n, unit, meanwhile=lambda: None):
                V.tensor_reduce(pk1[:, i:i + 1], peak[:, i, 0:n], X, ALU.max).then_inc(pk_part, 1)
                unit(sc[:, i, 0:1])
                link(V.tensor_scalar(sc[:, i, 1:2], sc[:, i, 0:1], 1.0 / QMAX, None, ALU.mult))
                meanwhile()
                dve.wait_ge(pk_all, i + 1)
                link(V.tensor_reduce(pkm[:, i:i + 1], ps_pk[:, 0:P], X, ALU.max))
                link(V.tensor_scalar(sc[:, i, 2:3], pkm[:, i:i + 1], sc[:, i, 1:2], TINY, ALU.mult, ALU.max))
                link(V.reciprocal(sc[:, i, 3:4], sc[:, i, 2:3]))
                V.tensor_scalar(sc[:, i, 4:5], sc[:, i, 3:4], sc[:, i, 0:1], None, ALU.mult).then_inc(scale_done, 1)
                dve.wait_ge(scale_done, i + 1)

            def block_peak(i, n, t):
                link(V.tensor_reduce(peak[:, i, n:n + 1], t, X, ALU.max, apply_absolute_value=True))

            dve.wait_ge(cond_T, 1)
            V.tensor_scalar(wcT[:, :], banks[0][:, 0:P], 1.0 / float(P) ** 0.5, None, ALU.mult).then_inc(cond_sb, 1)
            V.tensor_copy(yT[:, :], banks[0][:, P:P + B]).then_inc(cond_sb, 1)
            dve.wait_ge(cond_sb, 2)
            V.tensor_tensor(wc2[:, :], wcT[:, :], wcT[:, :], ALU.mult).then_inc(norm_in, 1)
            V.tensor_tensor(y2[:, :], yT[:, :], yT[:, :], ALU.mult).then_inc(norm_in, 1)
            for b in range(WY_V):
                V.tensor_scalar(wyT[:, b, :], wcT[:, :], yT[:, b:b + 1], None, ALU.mult).then_inc(wy_v, 1)
                if b == 5:
                    dve.wait_ge(norm_mm, 1)
                    V.tensor_scalar(nrm[:, 0, :], banks[1][:, 0:B], 1e-8, None, ALU.add).then_inc(norm_sb, 1)
            dve.wait_ge(norm_sb, 1)
            dve.wait_ge(root_done, 1)
            link(V.reciprocal(nrm[:, 2, :], nrm[:, 1, :]))
            link(V.tensor_tensor(nrm[:, 3, :], nrm[:, 2, :], nrm[:, 2, :], ALU.mult))
            link(V.scalar_tensor_tensor(nrm[:, 4, :], nrm[:, 3, :], -0.5, nrm[:, 0, :], ALU.mult, ALU.mult))
            link(V.tensor_scalar(nrm[:, 3, :], nrm[:, 4, :], 1.5, None, ALU.add))
            V.tensor_tensor(nrm[:, 1, :], nrm[:, 3, :], nrm[:, 2, :], ALU.mult).then_inc(norm_done, 1)
            dve.wait_ge(norm_done, 1)
            def weight_scales():
                dve.wait_ge(ld_w0, 48)
                wb = wn[:, :, :].rearrange("p n (k i) -> p (n k) i", i=WBLK)
                link(V.tensor_reduce(ws[:, 0, :], wb, X, ALU.max, apply_absolute_value=True))
                link(V.tensor_scalar(ws[:, 0, :], ws[:, 0, :], 1.0 / 7.0, TINY, ALU.mult, ALU.max))
                link(V.tensor_scalar(ws[:, 2, :], ws[:, 0, :], WS, None, ALU.mult))
                V.reciprocal(ws[:, 1, :], ws[:, 0, :]).then_inc(w_scales, 1)

            for k in range(NK):
                if k < C_V:
                    dve.wait_ge(c_mm, k + 1)
                    V.tensor_tensor(c32[:, 4 * k:4 * k + 4, :], batches(banks[k][:, :]),
                                    nrm[:, 1, 4 * k:4 * k + 4].unsqueeze(2).to_broadcast([P, 4, P]),
                                    ALU.mult).then_inc(c_v, 1)
                    dve.wait_ge(c_v, k + 1)
                else:
                    dve.wait_ge(c_s, k - C_V + 1)
                block_peak(0, k, c32[:, 4 * k:4 * k + 4, :].rearrange("p b l -> p (b l)"))
                if k == 0:
                    weight_scales()
            peak_to_scale(0, NK, lambda u: link(V.memset(u, 1.0)))
            for k in range(NK):
                ck = c32[:, 4 * k:4 * k + 4, :]
                if k in Q_HI_SCALAR:
                    dve.wait_ge(q_hi_s, Q_HI_SCALAR.index(k) + 1)
                else:
                    dve.wait_ge(cq_done, k + 1)
                    V.tensor_scalar(time_major(qhi, k), ck, -MAGIC, None, ALU.add).then_inc(q_hi_v, 1)
                    dve.wait_ge(q_hi_v, k + 1)
                V.scalar_tensor_tensor(time_major(qlo, k), ck, -MAGIC, time_major(qhi, k), ALU.add,
                                       ALU.subtract).then_inc(q_done, 1)
                for n in (0,) if k == 1 else (1, 2) if k == 3 else ():
                    dve.wait_ge(wT_hi_done, n + 1)
                    wj = slice(NJ * n, NJ * (n + 1))
                    V.tensor_tensor(wT_lo[:, wj, :].rearrange("p j o -> p (j o)"), banks[4 + n][:, 0:NJ * P],
                                    wT_hi[:, wj, :].rearrange("p j o -> p (j o)"), ALU.subtract).then_inc(wT_done, 1)

            def peak_gate_up(i, k):
                dve.wait_ge(gu_sb, (i - 1) * NJ * NK + NJ * (k + 1))
                link(V.tensor_reduce(peak[:, i, k:k + 1], tokens((gate2, up2)[i - 1], k), XY, ALU.max,
                                     apply_absolute_value=True))

            def round_sigmoid(n):
                dve.wait_ge(sig_done, n + 1)
                link(V.tensor_scalar(piece(sig2, n), piece(sig2, n), SIG_MAX, SIG_MAGIC, ALU.min, ALU.add))

            for i in (1, 2):
                for k in range(i - 1, NK):
                    peak_gate_up(i, k)
                    if i == 1 and k == 0:
                        dve.wait_ge(misc_T, 1)
                        V.tensor_copy(miscT[:, :], banks[3][:, 0:NM]).then_inc(misc_sb, 1)
                        dve.wait_ge(misc_sb, 1)
                        link(V.tensor_scalar(rw[:, :], miscT[:, SLOTS + 1:NM], WS, None, ALU.mult))
                        link(V.tensor_scalar(rw_hi[:, :], rw[:, :], 1.0, None, ALU.mult))
                        link(V.tensor_tensor(rw_lo[:, :], rw[:, :], rw_hi[:, :], ALU.subtract))
                peak_to_scale(i, NK, lambda u: link(V.tensor_scalar(u, sc[:, 0, 2:3], 1.0 / WS, None, ALU.mult)),
                              (lambda: peak_gate_up(2, 0)) if i == 1 else (lambda: round_sigmoid(0)))
            for n in range(SIG_PIECES):
                if n > 0:
                    round_sigmoid(n)
                V.tensor_tensor(piece(sig2, n), q16(piece(gate2, n)), q16(piece(sig2, n), U16), ALU.mult).then_inc(g2_done, 1)
                dve.wait_ge(g2_done, n + 1)
                block_peak(3, n, piece(sig2, n))
            peak_to_scale(3, SIG_PIECES, lambda u: link(V.tensor_scalar(u, sc[:, 1, 2:3], 1.0 / 65536.0, None, ALU.mult)))
            link(V.tensor_scalar(sixth(sig2, 0), sixth(sig2, 0), sc[:, 3, 4:5], MAGIC, ALU.mult, ALU.add))
            dve.wait_ge(upq, NJ)
            done = 0
            for n in range(2 * NJ):
                if n not in P_POOL:
                    if n > 0:
                        dve.wait_ge(g2q, n)
                    V.tensor_tensor(sixth(up2, n), q16(sixth(sig2, n)), q16(sixth(up2, n)), ALU.mult).then_inc(p_done, 1)
                    done += 1
                    dve.wait_ge(p_done, done)
                    block_peak(4, n, sixth(up2, n))
                for i, m in enumerate(P_POOL):
                    if n == PEAK_AFTER[i]:
                        dve.wait_ge(p_pool, i + 1)
                        block_peak(4, m, sixth(up2, m))
            peak_to_scale(4, 2 * NJ, lambda u: link(V.tensor_tensor(u, sc[:, 3, 2:3], sc[:, 2, 2:3], ALU.mult)))
            def quantise_o(c):
                V.tensor_scalar(chunk_of(up2, c), chunk_of(up2, c), sc[:, 4, 4:5], MAGIC, ALU.mult, ALU.add).then_inc(oq, 1)
                dve.wait_ge(oq, c + 1)
                V.tensor_scalar(chunk_of(o_hi, c), chunk_of(up2.bitcast(I8)[:, 1::4], c), 256.0, None,
                                ALU.mult).then_inc(o_hi_done, 1)

            def make_x1(c):
                at = slice(START[c], START[c + 1])
                dve.wait_ge(down_mm, c + 1)
                V.scalar_tensor_tensor(x1[:, at], banks[DOWN_BANKS[c]][:, 0:WIDTHS[c]], pk1[:, 0:1], xT[:, at], ALU.mult,
                                       ALU.add).then_inc(x1_done, 1)
                dve.wait_ge(x1_done, c + 1)
                V.tensor_copy(x1_hi[:, at], x1[:, at]).then_inc(x1_hi_done, 1)
                dve.wait_ge(x1_hi_done, c + 1)
                V.tensor_tensor(x1_lo[:, at], x1[:, at], x1_hi[:, at], ALU.subtract).then_inc(x1_lo_done, 1)

            for c in range(CH):
                quantise_o(c)
                if c == 0:
                    link(V.tensor_scalar(pk1[:, 0:1], sc[:, 4, 2:3], 1.0 / WS, None, ALU.mult))
                if c >= 3:
                    make_x1(c - 3)
            make_x1(CH - 3)
            V.tensor_copy(chunk_of(o_lo, CH - 1), chunk_of(up2.bitcast(U8)[:, 0::4], CH - 1)).then_inc(o_lo_v, 1)
            make_x1(CH - 2)
            make_x1(CH - 1)

            for n in range(GROUPS_BY[-1], GROUPS):
                dve.wait_ge(nat_T, n + 1)
                V.tensor_copy(wt[:, 1024 * n:1024 * (n + 1)], group_bank(n)).then_inc(wt_done, 1)

            def take_logits(c):
                dve.wait_ge(logits_mm, c + 1)
                V.tensor_copy(logit[:, 0:TILES[c], :].rearrange("p j e -> p (j e)"),
                              ps_logits[:, 0:TILES[c] * E]).then_inc(logit_sb, 1)

            def find_top(c):
                for j in range(TILES[c]):
                    V.max(top[:, j, :], logit[:, j, :]).then_inc(top_done, 1)

            def find_experts(c):
                V.tensor_tensor(mixd[:, 0, 0:TILES[c]], top[:, 0:TILES[c], 0], top[:, 0:TILES[c], 1], ALU.subtract).then_inc(margin_done, 1)
                for j in range(TILES[c]):
                    V.max_index(topi[:, j, :], top[:, j, :], logit[:, j, :]).then_inc(top_done, 1)

            def mark_experts(c):
                n = TILES[c]
                for a in range(2):
                    V.tensor_tensor(pick[:, a, 0:n, :], topi[:, 0:n, a:a + 1].to_broadcast([P, n, E]),
                                    experts[:, :].unsqueeze(1).to_broadcast([P, n, E]),
                                    ALU.is_equal).then_inc(pick_done, 1)

            def mix(c):
                n = TILES[c]
                dve.wait_ge(mix_done, c + 1)
                V.tensor_scalar(mixd[:, 2, 0:n], mixd[:, 1, 0:n], 0.5 / WS, 0.5 / WS, ALU.mult, ALU.add).then_inc(pick_done, 1)
                V.tensor_scalar(mixd[:, 3, 0:n], mixd[:, 1, 0:n], -0.5 / WS, 0.5 / WS, ALU.mult, ALU.add).then_inc(pick_done, 1)
                dve.wait_ge(pick_done, 6 * c + 4)
                for a in range(2):
                    V.tensor_tensor(pick[:, a, 0:n, :], pick[:, a, 0:n, :],
                                    mixd[:, 2 + a, 0:n].unsqueeze(2).to_broadcast([P, n, E]),
                                    ALU.mult).then_inc(pick_done, 1)
                dve.wait_ge(pick_done, 6 * c + 6)
                V.tensor_tensor(gates[:, START[c] // P:START[c + 1] // P, :], pick[:, 0, 0:n, :], pick[:, 1, 0:n, :],
                                ALU.add).then_inc(gates_done, 1)
                dve.wait_ge(gates_done, c + 1)

            def add_gated(c, e, j, par):
                tile = START[c] // P + j
                g = gates[:, tile:tile + 1, bass.ds(e, 1)].rearrange("p a b -> p (a b)")
                a = acc[:, tile, :]
                V.scalar_tensor_tensor(a, ps_y[par][:, P * j:P * (j + 1)], g, a, ALU.mult, ALU.add).then_inc(added, 1)

            def add_b2(c, left=0):
                dve.wait_ge(b2_summed, START[c + 1] // P)
                dve.wait_ge(added, NK + E * START[c + 1] // P - left * TILES[c])
                a = acc[:, START[c] // P:START[c + 1] // P, :]
                V.tensor_tensor(a, a, b2_sum[:, c % 2, 0:TILES[c], :], ALU.add).then_inc(b2_added, 1)

            def pair(c, e2, prev):
                first = is_first(e2)
                w = WIDTHS[c]
                for s in range(2 * NF):
                    f, par = s % NF, s // NF
                    slot = c * SLOTS + e2 * 2 * NF + s
                    if prev and f < 2:
                        cc, e = (c - 1, E - 2 + par) if first else (c, e2 * 2 - 2 + par)
                        if f == 0:
                            dve.wait_ge(y_mm, slot - NF)
                            dve.wait_ge(added, added_before(c, e2, par))
                        for j in (range(TILES[cc] // 2), range(TILES[cc] // 2, TILES[cc]))[f]:
                            add_gated(cc, e, j, par)
                    if first and s == 1:
                        take_logits(c)
                    if first and s == 7 and c > 0:
                        add_b2(c - 1)
                    if isinstance(e2, int) and not first and s == 6:
                        add_b2(c, 2)
                    if first and s == 2:
                        dve.wait_ge(logit_sb, c + 1)
                    if first and s == 3:
                        dve.wait_ge(top_done, 2 * START[c] // P + TILES[c])
                    if first and s == 4:
                        dve.wait_ge(top_done, 2 * START[c + 1] // P)
                    if first and s == 6:
                        mix(c)
                    if f not in HI_SCALAR[c]:
                        dve.wait_ge(g32_done, slot + 1)
                        V.tensor_copy(g_hi[:, par, f, 0:w], g32[:, f, 0:w]).then_inc(hi_v, 1)
                        dve.wait_ge(hi_v, hi_made(c, e2, s, False))
                    else:
                        dve.wait_ge(g_hi_done, hi_made(c, e2, s, True))
                    V.tensor_tensor(g_lo[:, par, f, 0:w], g32[:, f, 0:w], g_hi[:, par, f, 0:w],
                                    ALU.subtract).then_inc(g_lo_done, 1)
                    if first and s == 2:
                        find_top(c)
                    if first and s == 3:
                        find_experts(c)
                    if first and s == 4:
                        mark_experts(c)
            chunks(dve, pair)
            dve.wait_ge(b2_added, CH)
            for par in range(2):
                dve.wait_ge(y_mm, CH * SLOTS - NF + par * NF)
                dve.wait_ge(added, NK + E * TOK // P - (2 - par) * TILES[-1])
                for j in range(TILES[-1]):
                    add_gated(CH - 1, E - 2 + par, j, par)

        @block.tensor
        def _(pe):
            def mm(o, l, r, start, stop=True):
                return nc.tensor.matmul(o, l, r, start=start, stop=stop, skip_group_check=True)

            def mm3(o, l_hi, l_lo, r_hi, r_lo, start=True, r_lo_ready=None):
                mm(o, l_hi, r_hi, start)
                mm(o, l_lo, r_hi, False)
                if r_lo_ready:
                    pe.wait_ge(*r_lo_ready)
                return mm(o, l_hi, r_lo, False)

            def spread_peak(i):
                pe.wait_ge(pk_part, i + 1)
                mm(ps_pk[:, 0:P], pk1[:, i:i + 1].to_broadcast([P, P]), ident[:, :], True).then_inc(pk_all, 1)

            def transpose_group(n):
                if n % (GROUPS // 2) == 0:
                    pe.wait_ge(nat_done, 8 if n == 0 else 16)
                if n >= 2:
                    pe.wait_ge(wt_done, n - 1)
                for m in range(8):
                    last = nc.tensor.transpose(group_bank(n)[:, P * m:P * (m + 1)],
                                               nat[:, 1024 * n + P * m:1024 * n + P * (m + 1)], ident16[:, :])
                last.then_inc(nat_T, 1)

            pe.wait_ge(consts, 3)
            pe.wait_ge(ld_cond, 32)
            nc.tensor.transpose(banks[0][:, 0:P], wc[:, :], ident[:, :])
            nc.tensor.transpose(banks[0][:, P:P + B], y_sb[:, :], ident[0:B, 0:B]).then_inc(cond_T, 1)
            pe.wait_ge(norm_in, 2)
            mm(banks[1][:, 0:B], wc2[:, :], y2[:, :], True).then_inc(norm_mm, 1)
            for b in range(B):
                if b % 4 == 0:
                    pe.wait_ge(ld_x[b // 4], 16)
                if b == 4:
                    pe.wait_ge(norm_sb, 1)
                pe.wait_ge(*((wy_v, b + 1) if b < WY_V else (wy_s, b - WY_V + 1)))
                last = mm(banks[b // 4][:, P * (b % 4):P * (b % 4 + 1)], wyT[:, b, :], x_sb[:, b, :], True)
                if b % 4 == 3:
                    last.then_inc(c_mm, 1)
            for b in range(B):
                last = nc.tensor.transpose(banks[4 + b // 4][:, P * (b % 4):P * (b % 4 + 1)], x_sb[:, b, :], ident[:, :])
                if b % 4 == 3:
                    last.then_inc(xT_mm, 1)
            for k in range(NK):
                pe.wait_ge(*((c_v, k + 1) if k < C_V else (c_s, k - C_V + 1)))
                for b in range(4 * k, 4 * k + 4):
                    last = nc.tensor.transpose(banks[k][:, P * (b % 4):P * (b % 4 + 1)], c32[:, b, :], ident[:, :])
                last.then_inc(cT_mm, 1)
            pe.wait_ge(xT_sb, NK)
            spread_peak(0)
            for n in range(3):
                pe.wait_ge(wdeq, min(n, 1) + 1)
                for j in range(NJ):
                    last = nc.tensor.transpose(banks[4 + n][:, P * j:P * (j + 1)], wn[:, NJ * n + j, :], ident[:, :])
                last.then_inc(wT_mm, 1)
            for n in range(2 * NJ * NK):
                t, k, j = n // (NJ * NK), n % (NJ * NK) // NJ, n % NJ
                if n < NJ:
                    pe.wait_ge(wT_done, n + 1)
                if n == 0:
                    pe.wait_ge(q_hi_v, NK - len(Q_HI_SCALAR))
                    pe.wait_ge(q_hi_s, len(Q_HI_SCALAR))
                if n >= 6:
                    pe.wait_ge(gu_sb, n - 5)
                if n == NJ + 1:
                    pe.wait_ge(ld_misc, 48)
                    pe.wait_ge(cq_done, NK)
                    nc.tensor.transpose(banks[3][:, 0:NM], misc[:, :], ident[0:NM, 0:NM]).then_inc(misc_T, 1)
                if n == NJ * NK + 5:
                    spread_peak(1)
                w = NJ * t + j
                mm3(banks[GU_BANKS[n % 6]][:, :], wT_hi[:, w, :], wT_lo[:, w, :], blk(qhi, k), blk(qlo, k),
                    r_lo_ready=(q_done, NK) if n == 0 else None).then_inc(gu_mm, 1)
            pe.wait_ge(gu_sb, 2 * NJ * NK)
            spread_peak(2)
            for n in range(GROUPS_BY[0]):
                transpose_group(n)
            spread_peak(3)
            for n in range(GROUPS_BY[0], GROUPS_BY[-1]):
                transpose_group(n)
            spread_peak(4)

            def input_part(first, to):
                at = slice(B * first, B * to)
                mm3(ps_rnn[:, 0:B * (to - first)], wx_hi[:, :], wx_lo[:, :], x1_hi[:, at], x1_lo[:, at])

            w_h32 = wxh[:, 1, :]

            def first_step(r):
                if r:
                    pe.wait_ge(h32_done, r)
                state = h32[:, B * (r - 1):B * r] if r else yT[:, :]
                mm(ps_rnn[:, B * r:B * (r + 1)], w_h32, state, False).then_inc(rnn_mm, 1)

            for c in range(CH):
                if c == 2:
                    pe.wait_ge(small_w, 2)
                    pe.wait_ge(x1_lo_done, 1)
                    input_part(0, FIRST_STEPS)
                pe.wait_ge(o_hi_done, c + 1)
                for p, (part, w) in enumerate(((o_hi, wT_hi), (o_hi, wT_lo), (o_lo, wT_hi), (o_lo, wT_lo))):
                    if p == 2:
                        pe.wait_ge(*((o_lo_done, c + 1) if c < CH - 1 else (o_lo_v, 1)))
                    if c >= 2:
                        first_step((c - 2) * 4 + p)
                    for j in range(NJ):
                        last = mm(banks[DOWN_BANKS[c]][:, 0:WIDTHS[c]], w[:, 2 * NJ + j, :], chunk_of(part, c)[:, j, :],
                                  p == 0 and j == 0)
                last.then_inc(down_mm, 1)
            for k in range(NK):
                first_step(EARLY_STEPS + k)
                pe.wait_ge(x1_done, CH if k == NK - 1 else CH - 1)
                for j in range(4 * k, 4 * k + 4):
                    last = nc.tensor.transpose(banks[4 + k][:, P * (j % 4):P * (j % 4 + 1)], x1[:, P * j:P * (j + 1)], ident[:, :])
                last.then_inc(x1T_mm, 1)
                if k > 0:
                    transpose_group(GROUPS_BY[-1] + k - 1)
            for n in range(GROUPS_BY[-1] + NK - 1, GROUPS):
                transpose_group(n)

            def logits(c):
                for j in range(TILES[c]):
                    t = slice(START[c] + P * j, START[c] + P * (j + 1))
                    o = ps_logits[:, E * j:E * (j + 1)]
                    mm(o, h_hi[:, t], rw_hi[:, :], j == 0)
                    mm(o, h_hi[:, t], rw_lo[:, :], False)
                    mm(o, h_lo[:, t], rw_hi[:, :], False)
                    last = mm(o, h_lo[:, t], rw_lo[:, :], False)
                last.then_inc(logits_mm, 1)

            def down(e, par, f, tiles):
                w = bass.ds(e * FF + f * P, P)
                for j in range(tiles):
                    o = ps_y[par][:, P * j:P * (j + 1)]
                    tile = slice(P * j, P * (j + 1))
                    mm(o, g_hi[:, par, f, tile], w2T_hi[:, w], f == 0 and j == 0)
                    mm(o, g_hi[:, par, f, tile], w2T_lo[:, w], False)
                    last = mm(o, g_lo[:, par, f, tile], w2T_hi[:, w], False)
                last.then_inc(y_mm, 1)

            def pair(c, e2, prev):
                first = is_first(e2)
                for s in range(2 * NF):
                    f, par = s % NF, s // NF
                    slot = c * SLOTS + e2 * 2 * NF + s
                    if 0 < c < CH - 1 and first and s == 0:
                        pe.wait_ge(h32_done, RNN_FROM[c])
                        input_part(RNN_FROM[c], RNN_FROM[c + 1])
                    if prev or s >= NF:
                        e = e2 * 2 + par - 1 if not first else (E - 1 if par == 0 else 0)
                        tiles = TILES[c - 1] if first and par == 0 else TILES[c]
                        if c == 0 and first and f == 0:
                            pe.wait_ge(wt_done, GROUPS)
                        if f == 0 and prev:
                            pe.wait_ge(added, added_before(c, e2, par))
                        pe.wait_ge(g_lo_done, slot - NF + 1)
                        down(e, 1 - par, f, tiles)
                    step = rnn_step(c, e2, s)
                    if step is not None:
                        pe.wait_ge(h32_done, step)
                        mm(ps_rnn[:, bass.ds(rnn_column(c, step), B)], w_h32, h32[:, bass.ds((step - 1) * B, B)],
                           False).then_inc(rnn_mm, 1)
                    if first and s == 0:
                        pe.wait_ge(h_lo_done, START[c + 1] // (4 * B))
                    w = bass.ds(e2 * 2 * FF + s * P, P)
                    t = slice(START[c], START[c + 1])
                    mm3(ps_h[f][:, 0:WIDTHS[c]], w1T_hi[:, w], w1T_lo[:, w], h_hi[:, t], h_lo[:, t]).then_inc(hid_mm, 1)
                    if first and s == 0:
                        if prev:
                            pe.wait_ge(logit_sb, c)
                        logits(c)

            pe.wait_ge(h32_done, FIRST_STEPS)
            pe.wait_ge(x1_lo_done, CH)
            input_part(FIRST_STEPS, RNN_FROM[1])
            pe.wait_ge(added, NK)
            pe.wait_ge(wt_done, GROUPS // 2)
            chunks(pe, pair)
            pe.wait_ge(added, NK + E * TOK // P - 2 * TILES[-1])
            for f in range(NF):
                pe.wait_ge(g_lo_done, CH * SLOTS - NF + f + 1)
                down(E - 1, 1, f, TILES[-1])


def kernel(x, cond_1024, L0_cond_weight, L0_ffn_w_gate, L0_ffn_w_up, L0_ffn_w_down, L1_cond_Wx, L1_cond_Wh, L1_cond_b,
           L1_ffn_router_w, L1_ffn_w1, L1_ffn_b1, L1_ffn_w2, L1_ffn_b2):
    import numpy as np
    import concourse.bacc as bacc
    from concourse.bass_utils import run_bass_kernel_spmd

    nc = bacc.Bacc("TRN2", target_bir_lowering=False, num_devices=1)
    given = {"x": x, "cond": cond_1024, "w_cond": L0_cond_weight, "w_gate": L0_ffn_w_gate, "w_up": L0_ffn_w_up,
             "w_down": L0_ffn_w_down, "w_x": L1_cond_Wx, "w_h": L1_cond_Wh, "b_h": L1_cond_b,
             "w_router": L1_ffn_router_w, "w1": L1_ffn_w1, "b1": L1_ffn_b1, "w2": L1_ffn_w2, "b2": L1_ffn_b2}
    arrays = {f"in_{n}": np.ascontiguousarray(a) for n, a in given.items()}
    aps = [nc.dram_tensor(n, a.shape, mybir.dt.from_np(a.dtype), kind="ExternalInput").ap() for n, a in arrays.items()]
    out = nc.dram_tensor("out_block", x.shape, F32, kind="ExternalOutput").ap()
    program(nc, *aps, out)
    r = run_bass_kernel_spmd(nc, [arrays], core_ids=[0])
    return r.results[0]["out_block"]
```
